# Optimizing a Trainium2 kernel written in Bass

```python
import numpy as np
import jax
import jax.numpy as jnp

def _softmax(x, axis=-1):
    return jax.nn.softmax(x, axis=axis)

def _gelu(x):
    return jax.nn.gelu(x, approximate=True)

def _silu(x):
    return jax.nn.silu(x)

def _sigmoid(x):
    return jax.nn.sigmoid(x)

def _layernorm(x, axis=-1, eps=1e-05):
    m = jnp.mean(x, axis=axis, keepdims=True)
    v = jnp.var(x, axis=axis, keepdims=True)
    return (x - m) / jnp.sqrt(v + eps)

def _scatter_add(tgt, idx, src, axis=0):
    return tgt.at[idx].add(src)

def _segment_sum(src, seg, n):
    return jax.ops.segment_sum(src, seg, n)
kernel_name = 'mk_recurrent_d1_jaxref_r8_fd75f4'

def setup_inputs(seed: int=0):
    np.random.seed(seed)
    _w = jnp.asarray

    def _L0_attn_setup():
        import jax, jax.numpy as jnp
        import numpy as np
        D = 128
        H = 16
        KVH = 4
        HD = D // H
        LAT = 32
        WIN = 32
        B, S = (1, 256)
        BASE_G, BASE_L = (1000000.0, 10000.0)
        EPS = 1e-06

        def rmsnorm(x, w):
            return x * jax.lax.rsqrt(jnp.mean(x * x, axis=-1, keepdims=True) + EPS) * w

        def qk_norm(x):
            return x * jax.lax.rsqrt(jnp.mean(x * x, axis=-1, keepdims=True) + EPS)

        def rope(x, base):
            s, hd = (x.shape[-2], x.shape[-1])
            inv_freq = 1.0 / base ** (jnp.arange(0, hd, 2, dtype=jnp.float32) / hd)
            freqs = jnp.arange(s, dtype=jnp.float32)[:, None] * inv_freq[None, :]
            cos, sin = (jnp.cos(freqs), jnp.sin(freqs))
            xe, xo = (x[..., ::2], x[..., 1::2])
            out = jnp.stack([xe * cos - xo * sin, xe * sin + xo * cos], axis=-1)
            return out.reshape(x.shape)

        def split_heads(x, n_heads):
            b, s, _ = x.shape
            return x.reshape(b, s, n_heads, HD).transpose(0, 2, 1, 3)

        def repeat_kv(x):
            return jnp.repeat(x, H // KVH, axis=1)

        def sdpa(q, k, v, mask):
            scores = jnp.einsum('bhqd,bhkd->bhqk', q, k) / np.sqrt(HD).astype(np.float32)
            scores = jnp.where(mask, scores, jnp.float32(-1e+30))
            probs = jax.nn.softmax(scores, axis=-1)
            return jnp.einsum('bhqk,bhkd->bhqd', probs, v)

        def merge_heads(x):
            b, h, s, hd = x.shape
            return x.transpose(0, 2, 1, 3).reshape(b, s, h * hd)

        def global_latent_attn(x, wq, w_kv_down, w_k_up, w_v_up, wo):
            q = split_heads(x @ wq, H)
            latent = x @ w_kv_down
            k = split_heads(latent @ w_k_up, KVH)
            v = split_heads(latent @ w_v_up, KVH)
            q, k = (rope(q, BASE_G), rope(k, BASE_G))
            q, k = (qk_norm(q), qk_norm(k))
            k, v = (repeat_kv(k), repeat_kv(v))
            i = jnp.arange(x.shape[1])
            causal = i[:, None] >= i[None, :]
            return merge_heads(sdpa(q, k, v, causal)) @ wo

        def local_gqa_attn(x, wq, wk, wv, wo):
            q = split_heads(x @ wq, H)
            k = split_heads(x @ wk, KVH)
            v = split_heads(x @ wv, KVH)
            q, k = (rope(q, BASE_L), rope(k, BASE_L))
            q, k = (qk_norm(q), qk_norm(k))
            k, v = (repeat_kv(k), repeat_kv(v))
            i = jnp.arange(x.shape[1])
            diff = i[:, None] - i[None, :]
            mask = (diff >= 0) & (diff < WIN)
            return merge_heads(sdpa(q, k, v, mask)) @ wo
        key = jax.random.key(seed)
        ks = jax.random.split(key, 12)
        std = 0.02
        return {'hidden': jax.random.normal(ks[0], (B, S, D), dtype=jnp.float32), 'norm1_w': jnp.ones((D,), jnp.float32), 'norm2_w': jnp.ones((D,), jnp.float32), 'g_wq': jax.random.normal(ks[1], (D, H * HD), jnp.float32) * std, 'g_kv_down': jax.random.normal(ks[2], (D, LAT), jnp.float32) * std, 'g_k_up': jax.random.normal(ks[3], (LAT, KVH * HD), jnp.float32) * std, 'g_v_up': jax.random.normal(ks[4], (LAT, KVH * HD), jnp.float32) * std, 'g_wo': jax.random.normal(ks[5], (D, D), jnp.float32) * std, 'l_wq': jax.random.normal(ks[6], (D, H * HD), jnp.float32) * std, 'l_wk': jax.random.normal(ks[7], (D, KVH * HD), jnp.float32) * std, 'l_wv': jax.random.normal(ks[8], (D, KVH * HD), jnp.float32) * std, 'l_wo': jax.random.normal(ks[9], (D, D), jnp.float32) * std}
    _L0_attn_in = _L0_attn_setup()

    def _L0_ffn_setup():
        import jax, jax.numpy as jnp
        import numpy as np
        SWIGLU_ALPHA = 1.702
        SWIGLU_LIMIT = 7.0
        TOP_K = 4
        key = jax.random.key(seed)
        k = jax.random.split(key, 5)
        B, S, D, E, I = (2, 128, 128, 8, 256)
        return {'hidden_states': jax.random.normal(k[0], (B, S, D), dtype=jnp.float32), 'router_weight': jax.random.normal(k[1], (E, D), dtype=jnp.float32) * 0.02, 'router_bias': jnp.zeros((E,), dtype=jnp.float32), 'gate_up_proj': jax.random.normal(k[2], (E, 2 * I, D), dtype=jnp.float32) * 0.02, 'gate_up_proj_bias': jnp.zeros((E, 2 * I), dtype=jnp.float32), 'down_proj': jax.random.normal(k[3], (E, D, I), dtype=jnp.float32) * 0.02, 'down_proj_bias': jnp.zeros((E, D), dtype=jnp.float32)}
    _L0_ffn_in = _L0_ffn_setup()
    _d = {'L0_attn_hidden': _L0_attn_in['hidden'], 'L0_attn_norm1_w': _L0_attn_in['norm1_w'], 'L0_attn_norm2_w': _L0_attn_in['norm2_w'], 'L0_attn_g_wq': _L0_attn_in['g_wq'], 'L0_attn_g_kv_down': _L0_attn_in['g_kv_down'], 'L0_attn_g_k_up': _L0_attn_in['g_k_up'], 'L0_attn_g_v_up': _L0_attn_in['g_v_up'], 'L0_attn_g_wo': _L0_attn_in['g_wo'], 'L0_attn_l_wq': _L0_attn_in['l_wq'], 'L0_attn_l_wk': _L0_attn_in['l_wk'], 'L0_attn_l_wv': _L0_attn_in['l_wv'], 'L0_attn_l_wo': _L0_attn_in['l_wo'], 'L0_ffn_router_weight': _L0_ffn_in['router_weight'], 'L0_ffn_router_bias': _L0_ffn_in['router_bias'], 'L0_ffn_gate_up_proj': _L0_ffn_in['gate_up_proj'], 'L0_ffn_gate_up_proj_bias': _L0_ffn_in['gate_up_proj_bias'], 'L0_ffn_down_proj': _L0_ffn_in['down_proj'], 'L0_ffn_down_proj_bias': _L0_ffn_in['down_proj_bias']}
    _x0 = _d['L0_attn_hidden']
    _d['L0_attn_hidden'] = jax.random.normal(jax.random.fold_in(jax.random.key(seed), 1), (2, 1024, 128), dtype=_x0.dtype)
    del _x0
    return _d

def reference(L0_attn_hidden, L0_attn_norm1_w, L0_attn_norm2_w, L0_attn_g_wq, L0_attn_g_kv_down, L0_attn_g_k_up, L0_attn_g_v_up, L0_attn_g_wo, L0_attn_l_wq, L0_attn_l_wk, L0_attn_l_wv, L0_attn_l_wo, L0_ffn_router_weight, L0_ffn_router_bias, L0_ffn_gate_up_proj, L0_ffn_gate_up_proj_bias, L0_ffn_down_proj, L0_ffn_down_proj_bias):

    def _L0_attn_ref(hidden, norm1_w, norm2_w, g_wq, g_kv_down, g_k_up, g_v_up, g_wo, l_wq, l_wk, l_wv, l_wo):
        import jax, jax.numpy as jnp
        import numpy as np
        D = 128
        H = 16
        KVH = 4
        HD = D // H
        LAT = 32
        WIN = 32
        B, S = (1, 256)
        BASE_G, BASE_L = (1000000.0, 10000.0)
        EPS = 1e-06

        def rmsnorm(x, w):
            return x * jax.lax.rsqrt(jnp.mean(x * x, axis=-1, keepdims=True) + EPS) * w

        def qk_norm(x):
            return x * jax.lax.rsqrt(jnp.mean(x * x, axis=-1, keepdims=True) + EPS)

        def rope(x, base):
            s, hd = (x.shape[-2], x.shape[-1])
            inv_freq = 1.0 / base ** (jnp.arange(0, hd, 2, dtype=jnp.float32) / hd)
            freqs = jnp.arange(s, dtype=jnp.float32)[:, None] * inv_freq[None, :]
            cos, sin = (jnp.cos(freqs), jnp.sin(freqs))
            xe, xo = (x[..., ::2], x[..., 1::2])
            out = jnp.stack([xe * cos - xo * sin, xe * sin + xo * cos], axis=-1)
            return out.reshape(x.shape)

        def split_heads(x, n_heads):
            b, s, _ = x.shape
            return x.reshape(b, s, n_heads, HD).transpose(0, 2, 1, 3)

        def repeat_kv(x):
            return jnp.repeat(x, H // KVH, axis=1)

        def sdpa(q, k, v, mask):
            scores = jnp.einsum('bhqd,bhkd->bhqk', q, k) / np.sqrt(HD).astype(np.float32)
            scores = jnp.where(mask, scores, jnp.float32(-1e+30))
            probs = jax.nn.softmax(scores, axis=-1)
            return jnp.einsum('bhqk,bhkd->bhqd', probs, v)

        def merge_heads(x):
            b, h, s, hd = x.shape
            return x.transpose(0, 2, 1, 3).reshape(b, s, h * hd)

        def global_latent_attn(x, wq, w_kv_down, w_k_up, w_v_up, wo):
            q = split_heads(x @ wq, H)
            latent = x @ w_kv_down
            k = split_heads(latent @ w_k_up, KVH)
            v = split_heads(latent @ w_v_up, KVH)
            q, k = (rope(q, BASE_G), rope(k, BASE_G))
            q, k = (qk_norm(q), qk_norm(k))
            k, v = (repeat_kv(k), repeat_kv(v))
            i = jnp.arange(x.shape[1])
            causal = i[:, None] >= i[None, :]
            return merge_heads(sdpa(q, k, v, causal)) @ wo

        def local_gqa_attn(x, wq, wk, wv, wo):
            q = split_heads(x @ wq, H)
            k = split_heads(x @ wk, KVH)
            v = split_heads(x @ wv, KVH)
            q, k = (rope(q, BASE_L), rope(k, BASE_L))
            q, k = (qk_norm(q), qk_norm(k))
            k, v = (repeat_kv(k), repeat_kv(v))
            i = jnp.arange(x.shape[1])
            diff = i[:, None] - i[None, :]
            mask = (diff >= 0) & (diff < WIN)
            return merge_heads(sdpa(q, k, v, mask)) @ wo
        x = hidden
        x = x + global_latent_attn(rmsnorm(x, norm1_w), g_wq, g_kv_down, g_k_up, g_v_up, g_wo)
        x = x + local_gqa_attn(rmsnorm(x, norm2_w), l_wq, l_wk, l_wv, l_wo)
        return x

    def _L0_ffn_ref(hidden_states, router_weight, router_bias, gate_up_proj, gate_up_proj_bias, down_proj, down_proj_bias):
        import jax, jax.numpy as jnp
        import numpy as np
        SWIGLU_ALPHA = 1.702
        SWIGLU_LIMIT = 7.0
        TOP_K = 4
        B, S, D = hidden_states.shape
        E = router_weight.shape[0]
        x = hidden_states.reshape(-1, D)
        N = x.shape[0]
        logits = x @ router_weight.T + router_bias
        topk_logits, topk_idx = jax.lax.top_k(logits, TOP_K)
        topk_w = jax.nn.softmax(topk_logits.astype(jnp.float32), axis=-1)
        combine = jnp.zeros((N, E), dtype=jnp.float32)
        combine = combine.at[jnp.arange(N)[:, None], topk_idx].set(topk_w)
        gate_up = jnp.einsum('nd,ejd->nej', x, gate_up_proj) + gate_up_proj_bias
        gate, up = jnp.split(gate_up, 2, axis=-1)
        gate = jnp.minimum(gate, SWIGLU_LIMIT)
        up = jnp.clip(up, -SWIGLU_LIMIT, SWIGLU_LIMIT)
        act = (up + 1.0) * gate * jax.nn.sigmoid(SWIGLU_ALPHA * gate)
        out = jnp.einsum('nei,edi->ned', act, down_proj) + down_proj_bias
        y = jnp.einsum('ned,ne->nd', out, combine.astype(out.dtype))
        return y.reshape(B, S, D)
    x = L0_attn_hidden
    xn = _layernorm(x, axis=-1)
    s = _L0_attn_ref(xn, L0_attn_norm1_w, L0_attn_norm2_w, L0_attn_g_wq, L0_attn_g_kv_down, L0_attn_g_k_up, L0_attn_g_v_up, L0_attn_g_wo, L0_attn_l_wq, L0_attn_l_wk, L0_attn_l_wv, L0_attn_l_wo)
    g = _silu(_L0_ffn_ref(xn, L0_ffn_router_weight, L0_ffn_router_bias, L0_ffn_gate_up_proj, L0_ffn_gate_up_proj_bias, L0_ffn_down_proj, L0_ffn_down_proj_bias))
    x = x + s * g
    return x

_drawn_inputs = setup_inputs


def setup_inputs(seed=0):
    import zlib

    import numpy as np

    out = dict(_drawn_inputs(seed))
    spreads = {'L0_attn_norm1_w': (1.0, 0.6),
     'L0_attn_norm2_w': (1.0, 0.6),
     'L0_ffn_router_bias': (0.0, 0.649),
     'L0_ffn_gate_up_proj_bias': (0.0, 0.8),
     'L0_ffn_down_proj_bias': (0.0, 0.337)}
    factors = {'L0_attn_g_wq': 8.0,
     'L0_attn_g_kv_down': 8.0,
     'L0_attn_g_k_up': 8.0,
     'L0_attn_g_v_up': 8.0,
     'L0_attn_g_wo': 8.0,
     'L0_attn_l_wq': 8.0,
     'L0_attn_l_wk': 8.0,
     'L0_attn_l_wv': 8.0,
     'L0_attn_l_wo': 8.0,
     'L0_ffn_router_weight': 2.982,
     'L0_ffn_gate_up_proj': 5.684,
     'L0_ffn_down_proj': 5.196}
    for name, (base, spread) in spreads.items():
        noise = np.random.default_rng([zlib.crc32(name.encode()), seed]).standard_normal(out[name].shape)
        drawn = base * np.exp(spread * noise) if base else spread * noise
        out[name] = jnp.asarray(drawn.astype(out[name].dtype))
    for name, factor in factors.items():
        out[name] = (out[name] * factor).astype(out[name].dtype)
    return out
```

```python
import concourse.bass as bass
from concourse import mybir
from contextlib import ExitStack

B, S, D = 2, 1024, 128
T = S // 128
H, KVH, HD = 16, 4, 8
J = H // KVH
WIN = 32
E, I = 8, 256
TOPK = 4
LIMIT, ALPHA = 7.0, 1.702
LN_EPS, RMS_EPS = 1e-5, 1e-6
HEADS = H + KVH
QK = HEADS * HD
PROJ = QK + KVH * HD
PARTS = 4
QKSCALE = 64.0
EXP_SCALE = 1.0 / (QKSCALE * QKSCALE * HD ** 0.5)
MAGIC = float(0x5F3759DF)
CH = 512
NCH = S // CH
IT = I // 128
FU = NCH * E


def gated_attention_moe_kernel(nc, hidden, n1, n2, g_wq, g_kvd, g_ku, g_vu, g_wo, l_wq, l_wk, l_wv, l_wo,
                               r_w, r_b, gu_w, gu_b, dn_w, dn_b, c32, c16, out):
    fp32, fp16, i32 = mybir.dt.float32, mybir.dt.float16, mybir.dt.int32
    ALU = mybir.AluOpType
    ACT = mybir.ActivationFunctionType
    AXX = mybir.AxisListType.X

    G_UNITS = [("g", t, kt) for t in range(T) for kt in [t] + list(range(t))]
    L_UNITS = [("l", t, t) for t in range(T)]
    UNITS = G_UNITS + L_UNITS
    NU = len(UNITS)
    JOBS = []
    for u, (ph, t, kt) in enumerate(UNITS):
        JOBS += [(u, 0), (u, 1)]
        if ph == "l" and t > 0:
            JOBS.append((u, 2))
    NJ = len(JOBS)
    JOB = {j: n for n, j in enumerate(JOBS)}
    MASKED = [u for u, (ph, t, kt) in enumerate(UNITS) if kt == t]
    MASKJOBS = [j for j in JOBS if j[0] in MASKED]
    MJ = {j: n for n, j in enumerate(MASKJOBS)}
    LAST = [u for u, (ph, t, kt) in enumerate(UNITS) if u + 1 == NU or UNITS[u + 1][:2] != (ph, t)]
    POST = {u: n for n, u in enumerate(LAST)}
    NP = len(LAST)

    ctx = ExitStack()
    with ctx:
        def sb(name, shape, dt=fp32):
            return ctx.enter_context(nc.sbuf_tensor(name, shape, dt))

        def sem(name):
            return ctx.enter_context(nc.semaphore(name))

        k32 = sb("k32", [128, c32.shape[1]])
        ident = k32[:, 0:128]
        earlier = k32[:, 128:192]
        rope = {"g": k32[:, 192:320], "l": k32[:, 320:448]}
        k16 = sb("k16", [128, 128], fp16)
        wq_in = {"g": sb("wq_g", [128, H * HD]), "l": sb("wq_l", [128, H * HD])}
        wkv_in = sb("wkv_in", [128, 2 * KVH * HD])
        kvd = sb("kvd", [128, 32])
        kvdT = sb("kvdT", [32, 128])
        kvu = sb("kvu", [32, 2 * KVH * HD])
        norm_w = {"g": sb("n1w", [128, 1]), "l": sb("n2w", [128, 1])}
        wproj = {"g": sb("wproj_g", [128, PROJ]), "l": sb("wproj_l", [128, PROJ])}
        wo = {"g": sb("wo_g", [128, D]), "l": sb("wo_l", [128, D])}
        rw_in = sb("rw_in", [E, D])
        rwT = sb("rwT", [128, E])
        rb = sb("rb", [128, E])
        gub_in = sb("gub_in", [4 * E, 128])
        gub = sb("gub", [128, E, 2 * IT])
        guT = sb("guT", [128, 4 * E, 128])
        dnT = sb("dnT", [128, 2 * E, D])
        dnb = sb("dnb", [E, D])

        xs = sb("xs", [128, T, D])
        xn = sb("xn", [128, T, D])
        x1 = sb("x1", [128, T, D])
        ss = sb("ss", [128, T, D])
        xT = {"g": sb("xnT", [128, S]), "l": sb("x1T", [128, S])}
        stats = sb("stats", [128, T, 6])
        mv = sb("mv", [128, T, 2])
        rs = sb("rs", [128, 4, T])
        ntmp = sb("ntmp", [128, 2, T * HEADS])
        qk = sb("qk", [128, T * HEADS, HD])
        rot = sb("rot", [128, T * HEADS, HD])
        rtmp = sb("rtmp", [128, T * HEADS, HD])
        msq = sb("msq", [128, T * HEADS])
        rn = sb("rn", [128, T * HEADS])
        stk = sb("stk", [128, T * HEADS, PARTS, HD], fp16)
        qT = sb("qT", [128, T, J * 128], fp16)
        kz = sb("kz", [128, KVH, S], fp16)
        v = sb("v", [128, T, KVH, 32])
        P = sb("P", [128, 3, 4 * 512])
        Pp = sb("Pp", [128, 2, 512])
        oT = sb("oT", [128, 2, 512])
        on = sb("on", [128, 2, 128])
        onT = sb("onT", [128, 2, 128])
        rec = sb("rec", [128, 2, H])
        lg = sb("lg", [128, T, E])
        pair = sb("pair", [128, 2, T * E * E])
        rank = sb("rank", [128, T * E])
        cw = sb("cw", [128, T, E])
        mx = sb("mx", [128, 2, T])
        wT = sb("wT", [E, S])
        wb = sb("wb", [128, E * S])
        gate = sb("gate", [128, 2, IT * CH])
        sig = sb("sig", [128, 2, IT * CH])
        up = sb("up", [128, 2, IT * CH])
        yT, yth = oT[:, 0, :], oT[:, 1, :]
        ys = sb("ys", [128, T, D])
        aw = P[:, 0, :].rearrange("p (n c) -> p n c", n=2)
        gu_in = wb[:, 0:4096].rearrange("p (m d) -> p m d", d=128)
        dn_in = wb[:, 4096:6144].rearrange("p (e i) -> p e i", i=I)

        SP_ = ctx.enter_context(nc.psum_tensor("scores", [128, 2048], fp32))
        OP = ctx.enter_context(nc.psum_tensor("outs", [128, 1024], fp32))
        MP = ctx.enter_context(nc.psum_tensor("misc", [128, 1024], fp32))
        M0, M1 = MP[:, 0:512], MP[:, 512:1024]

        w_dram = nc.dram_tensor("combine_rows", [B, E, S], fp32, kind="Internal").ap()

        s_att = sem("attn_inputs_loaded")
        s_ffn = sem("ffn_inputs_loaded")
        s_zero = sem("pads_written")
        s_pw = sem("prep_product")
        s_pe_ = sem("prep_evacuated")
        s_tp = sem("ffn_weight_transposed")
        s_te = sem("ffn_weight_evacuated")
        s_x = sem("x_loaded")
        s_link = sem("vector_step")
        s_plink = sem("pool_step")
        s_xn = sem("normed")
        s_xtp = sem("x_transposed")
        s_xts = sem("xT_written")
        s_prj = sem("projected")
        s_pev = sem("projection_evacuated")
        s_cos = sem("rope_cos_done")
        s_rot = sem("rotated")
        s_sq = sem("squares_done")
        s_stk = sem("parts_stacked")
        s_qkt = sem("qk_transposed")
        s_qTs = sem("qT_written")
        s_kTs = sem("kT_written")
        s_lg = sem("logits_done")
        s_lx = sem("logits_shifted")
        s_le = sem("logits_exp")
        s_cw = sem("combine_done")
        s_wtp = sem("combine_transposed")
        s_wts = sem("wT_written")
        s_wst = sem("combine_stored")
        s_wb = sem("combine_broadcast")
        s_sc = sem("scores_done")
        s_ex = sem("exp_done")
        s_mk = sem("masked")
        s_pv = sem("pv_done")
        s_o = sem("o_evacuated")
        s_ot = sem("o_transposed")
        s_on = sem("o_normalised")
        s_ont = sem("on_transposed")
        s_ons = sem("onT_written")
        s_wo = sem("wo_done")
        s_x1 = sem("residual_added")
        s_g = sem("gate_done")
        s_u = sem("up_done")
        s_gs = sem("gate_evacuated")
        s_th = sem("tanh_done")
        s_us = sem("up_evacuated")
        s_uc = sem("up_clipped")
        s_a = sem("act_done")
        s_aw = sem("act_weighted")
        s_dn = sem("down_done")
        s_ys = sem("y_evacuated")
        s_yt = sem("y_transposed")
        s_yth = sem("y_tanh")
        s_out = sem("result_ready")
        s_st = sem("result_stored")
        s_pass = {"pool": sem("pool_passed"), "dve": sem("vector_passed"), "sp": sem("sync_passed")}

        block = ctx.enter_context(nc.Block())

        def pair_of(job):
            n = JOB[job] % 2
            return SP_[:, n * 1024:(n + 1) * 1024]

        @block.sync
        def _(sp):
            for done in (s_out, s_aw, s_gs, s_us, s_u, s_dn):
                sp.sem_inc(done, 1)
            for done in (s_wst, s_st):
                sp.sem_inc(done, 16)
            for dst, src in ((k32[:, :], c32), (k16[:, :], c16), (wq_in["g"][:, :], g_wq), (kvd[:, :], g_kvd),
                             (kvu[:, 0:32], g_ku), (kvu[:, 32:64], g_vu), (wo["g"][:, :], g_wo),
                             (wq_in["l"][:, :], l_wq), (wkv_in[:, 0:32], l_wk), (wkv_in[:, 32:64], l_wv),
                             (wo["l"][:, :], l_wo), (norm_w["g"][:, :], n1.rearrange("(p o) -> p o", o=1)),
                             (norm_w["l"][:, :], n2.rearrange("(p o) -> p o", o=1))):
                sp.dma_start(dst, src).then_inc(s_att, 16)
            for dst, src in ((rw_in[:, :], r_w), (rb[:, :], r_b.rearrange("(o e) -> o e", o=1).to_broadcast([128, E])),
                             (gub_in[:, :], gu_b.rearrange("e (m j) -> (e m) j", j=128)), (dnb[:, :], dn_b),
                             (gu_in, gu_w.rearrange("e (m j) d -> j (e m) d", j=128)),
                             (dn_in, dn_w.rearrange("e d i -> d e i"))):
                sp.dma_start(dst, src).then_inc(s_ffn, 16)
            with sp.Fori(0, B) as b:
                sp.wait_ge(s_out, 1 + b * NCH)
                sp.sem_inc(s_pass["sp"], 1)
                sp.dma_start(xs[:, :, :], hidden[bass.ds(b, 1), :, :].rearrange("o (t p) d -> p (o t) d", p=128)) \
                    .then_inc(s_x, 16)
                sp.wait_ge(s_wts, b + 1)
                sp.sem_inc(s_pass["sp"], 1)
                sp.dma_start(w_dram[bass.ds(b, 1), :, :].rearrange("o e s -> (o e) s"), wT[:, :]).then_inc(s_wst, 16)
                sp.wait_ge(s_wst, 16 + b * 16 + 16)
                sp.sem_inc(s_pass["sp"], 1)
                sp.wait_ge(s_aw, 1 + b * FU)
                sp.sem_inc(s_pass["sp"], 1)
                sp.wait_ge(s_te, 12)
                sp.sem_inc(s_pass["sp"], 1)
                sp.dma_start(wb[:, :], w_dram[bass.ds(b, 1), :, :].rearrange("o e s -> o (e s)")
                             .to_broadcast([128, E * S])).then_inc(s_wb, 16)
                for c in range(NCH):
                    sp.wait_ge(s_out, 1 + b * NCH + c + 1)
                    sp.sem_inc(s_pass["sp"], 1)
                    sp.dma_start(out[bass.ds(b, 1), c * CH:(c + 1) * CH, :].rearrange("o (t p) d -> p (o t) d", p=128),
                                 ys[:, c * CH // 128:(c + 1) * CH // 128, :]).then_inc(s_st, 16)
            sp.wait_ge(s_st, 16 + B * NCH * 16)

        @block.tensor
        def _(pe):
            pe.wait_ge(s_att, 13 * 16)
            nc.tensor.transpose(M0[0:32, 0:128], kvd[:, :], ident).then_inc(s_pw, 1)
            pe.wait_ge(s_pe_, 1)
            nc.tensor.matmul(M0[:, 128:192], kvdT[:, :], kvu[:, :], start=True, stop=True).then_inc(s_pw, 1)
            pe.wait_ge(s_ffn, 6 * 16)
            nc.tensor.transpose(M1[:, 0:E], rw_in[:, :], ident[0:E, 0:E])
            nc.tensor.transpose(M1[:, 64:64 + 4 * E], gub_in[:, :], ident[0:4 * E, 0:4 * E]).then_inc(s_pw, 1)
            for n in range(12):
                if n >= 4:
                    pe.wait_ge(s_te, n - 3)
                for i in range(4):
                    m = 4 * n + i
                    src = gu_in[:, m, :] if m < 32 else dn_in[:, (m - 32) // 2, ((m - 32) % 2) * 128:((m - 32) % 2 + 1) * 128]
                    last = nc.tensor.transpose(SP_[:, (n % 4) * 512 + i * 128:(n % 4) * 512 + (i + 1) * 128], src, ident)
                last.then_inc(s_tp, 1)

            def qkv(b, ph):
                f = 0 if ph == "g" else 1
                x = xn if ph == "g" else x1
                if ph == "g":
                    pe.wait_ge(s_xn, b + 1)
                    pe.wait_ge(s_te, 12)
                    pe.wait_ge(s_gs, 1 + b * FU)
                else:
                    pe.wait_ge(s_x1, b * NP + T)
                for h in range(2):
                    for i in range(4):
                        last = nc.tensor.transpose(SP_[:, h * 512 + i * 128:h * 512 + (i + 1) * 128], x[:, 4 * h + i, :], ident)
                    last.then_inc(s_xtp, 1)
                pe.wait_ge(s_xts, b * 4 + 2 * f + 2)
                if ph == "g":
                    pe.wait_ge(s_out, 1 + b * NCH)
                    pe.wait_ge(s_pe_, 5)
                banks = [SP_[:, 1024:1536], SP_[:, 1536:2048], M0, M1]
                for h in range(4):
                    for i in range(2):
                        last = nc.tensor.matmul(banks[h][:, i * PROJ:(i + 1) * PROJ], xT[ph][:, (2 * h + i) * 128:(2 * h + i + 1) * 128],
                                                wproj[ph][:, :], start=True, stop=True)
                    last.then_inc(s_prj, 1)
                if ph == "g":
                    pe.wait_ge(s_us, 1 + b * FU)
                    for t in range(T):
                        last = nc.tensor.matmul(OP[:, t * E:(t + 1) * E], xT[ph][:, t * 128:(t + 1) * 128], rwT[:, :],
                                                start=True, stop=True)
                    last.then_inc(s_lg, 1)
                    pe.wait_ge(s_cw, b + 1)
                    for t in range(T):
                        last = nc.tensor.transpose(OP[0:E, t * 128:(t + 1) * 128], cw[:, t, :], ident)
                    last.then_inc(s_wtp, 1)
                pe.wait_ge(s_stk, b * 2 + f + 1)
                for h in range(4):
                    bank = SP_[:, h * 512:(h + 1) * 512].bitcast(fp16)
                    for i in range(2):
                        t = 2 * h + i
                        for j in range(J):
                            at = i * 512 + j * 128
                            hh = t * HEADS + j * KVH
                            last = nc.tensor.transpose(bank[:, at:at + 128], stk[:, hh:hh + KVH, :, :].rearrange("p a b d -> p (a b d)"), k16[:, :])
                    last.then_inc(s_qkt, 1)
                bank = M0.bitcast(fp16)
                for t in range(T):
                    hh = t * HEADS + H
                    last = nc.tensor.transpose(bank[:, t * 128:(t + 1) * 128], stk[:, hh:hh + KVH, :, :].rearrange("p a b d -> p (a b d)"), k16[:, :])
                last.then_inc(s_qkt, 1)

            def scores(b, job):
                u, part = job
                ph, t, kt = UNITS[u]
                n = JOB[job]
                s = pair_of(job)
                if part == 0 and u in (0, len(G_UNITS)):
                    f = 0 if u == 0 else 1
                    pe.wait_ge(s_qTs, b * 8 + 4 * f + 4)
                    pe.wait_ge(s_kTs, b * 2 + f + 1)
                if n >= 2:
                    pe.wait_ge(s_ex, b * NJ + n - 1)
                if part < 2:
                    for c in (2 * part, 2 * part + 1):
                        last = nc.tensor.matmul(s[:, (c % 2) * 512:(c % 2 + 1) * 512], kz[:, c, kt * 128:(kt + 1) * 128],
                                                qT[:, t, :], start=True, stop=True)
                else:
                    q = qT[:, t, :].rearrange("p (j q) -> p j q", q=128)[:, :, 0:WIN]
                    for c in range(KVH):
                        last = nc.tensor.matmul(s[128 - WIN:128, c * 128:(c + 1) * 128], kz[:, c, t * 128 - WIN:t * 128], q,
                                                start=True, stop=True)
                last.then_inc(s_sc, 1)

            def pv(b, u):
                ph, t, kt = UNITS[u]
                ends = POST.get(u)
                p = sum(1 for w in LAST if w < u)
                first = u == 0 or (u - 1) in POST
                if first:
                    if p >= 2:
                        pe.wait_ge(s_o, b * NP + p - 1)
                    else:
                        pe.wait_ge(s_wts, b + 1)
                has_prev = ph == "l" and t > 0
                pe.wait_ge(s_ex, b * NJ + JOB[(u, 2 if has_prev else 1)] + 1)
                if kt == t:
                    pe.wait_ge(s_mk, b * len(MJ) + MJ[(u, 2 if has_prev else 1)] + 1)
                o = OP[:, (p % 2) * 512:(p % 2 + 1) * 512]
                for c in range(KVH):
                    last = nc.tensor.matmul(o[32 * c:32 * c + 32, :], v[:, kt, c, :], P[:, u % 3, c * 512:(c + 1) * 512],
                                            start=first, stop=ends is not None and not has_prev)
                if has_prev:
                    for c in range(KVH):
                        last = nc.tensor.matmul(o[32 * c:32 * c + 32, :].rearrange("p (j q) -> p j q", q=128)[:, :, 0:WIN],
                                                v[:, t - 1, c, :], Pp[:, t % 2, c * 128:(c + 1) * 128], start=False, stop=True)
                last.then_inc(s_pv, 1)

            def post_a(b, p):
                pe.wait_ge(s_o, b * NP + p + 1)
                if p >= 1:
                    pe.wait_ge(s_on, b * NP + p)
                for j in range(J):
                    last = nc.tensor.transpose(M0[:, j * 128:(j + 1) * 128], oT[:, p % 2, j * 128:(j + 1) * 128], ident)
                last.then_inc(s_ot, 1)

            def post_b(b, p):
                pe.wait_ge(s_on, b * NP + p + 1)
                added = sum(1 for w in LAST if w + 4 < LAST[p] + 3 and (w < len(G_UNITS)) == (p < T)) + (T if p >= T else 0)
                if added:
                    pe.wait_ge(s_x1, b * NP + added)
                nc.tensor.transpose(M1[:, 0:128], on[:, p % 2, :], ident).then_inc(s_ont, 1)

            def post_c(b, p, ph, newer):
                pe.wait_ge(s_ons, b * NP + newer + 1)
                if p >= 1:
                    pe.wait_ge(s_x1, b * NP + p)
                nc.tensor.matmul(M1[:, 128:256], onT[:, p % 2, :], wo[ph][:, :], start=True, stop=True).then_inc(s_wo, 1)

            def stream(b, units):
                first, end = units[0], units[-1] + 1
                jobs = {u: [j for j in JOBS if j[0] == u] for u in units}
                for j in jobs[first]:
                    scores(b, j)
                for u in range(first, end + 4):
                    if u - 2 in POST and first <= u - 2 < end:
                        post_a(b, POST[u - 2])
                    if u - 3 in POST and first <= u - 3 < end:
                        post_b(b, POST[u - 3])
                    nxt = jobs.get(u + 1, [])
                    for j in nxt[:1]:
                        scores(b, j)
                    if u - 4 in POST and first <= u - 4 < end:
                        newer = POST[u - 3] if u - 3 in POST and u - 3 < end else POST[u - 4]
                        post_c(b, POST[u - 4], UNITS[u - 4][0], newer)
                    if first <= u - 1 < end:
                        pv(b, u - 1)
                    for j in nxt[1:]:
                        scores(b, j)

            def ffn(b):
                def hidden_unit(n):
                    ch, e = divmod(n, E)
                    x = xT["g"][:, ch * CH:(ch + 1) * CH]
                    if n >= 2:
                        pe.wait_ge(s_gs, 1 + b * FU + n - 1)
                    for i in range(IT):
                        last = nc.tensor.matmul(SP_[:, (n % 2) * 1024 + i * CH:(n % 2) * 1024 + (i + 1) * CH],
                                                guT[:, 4 * e + i, :], x, start=True, stop=True)
                    last.then_inc(s_g, 1)
                    if n >= 1:
                        pe.wait_ge(s_us, 1 + b * FU + n)
                    for i in range(IT):
                        last = nc.tensor.matmul(OP[:, i * CH:(i + 1) * CH], guT[:, 4 * e + IT + i, :], x, start=True, stop=True)
                    last.then_inc(s_u, 1)

                def down(n):
                    ch, e = divmod(n, E)
                    y = (M0, M1)[ch]
                    pe.wait_ge(s_aw, 1 + b * FU + n + 1)
                    for i in range(IT):
                        last = nc.tensor.matmul(y, dnT[:, 2 * e + i, :], aw[:, n % 2, i * CH:(i + 1) * CH],
                                                start=(e == 0 and i == 0), stop=False)
                    last.then_inc(s_dn, 1)
                    if e == E - 1:
                        nc.tensor.matmul(y, dnb[:, :], wT[:, ch * CH:(ch + 1) * CH], start=False, stop=True).then_inc(s_dn, 1)

                pe.wait_ge(s_x1, b * NP + NP)
                hidden_unit(0)
                for n in range(FU):
                    if n + 1 < FU:
                        hidden_unit(n + 1)
                    down(n)
                    if n % E == 2 and n >= E:
                        y_back(b, n // E - 1)
                y_back(b, NCH - 1)

            def y_back(b, ch):
                pe.wait_ge(s_ys, b * NCH + ch + 1)
                for i in range(4):
                    last = nc.tensor.transpose((M0, M1)[ch][:, i * 128:(i + 1) * 128], yT[:, i * 128:(i + 1) * 128], ident)
                last.then_inc(s_yt, 1)

            with pe.Fori(0, B) as b:
                qkv(b, "g")
                stream(b, range(0, len(G_UNITS)))
                qkv(b, "l")
                stream(b, range(len(G_UNITS), NU))
                ffn(b)

        @block.scalar
        def _(act):
            for n in range(12):
                act.wait_ge(s_tp, n + 1)
                src = SP_[:, (n % 4) * 512:(n % 4 + 1) * 512]
                if n < 8:
                    nc.scalar.activation(guT[:, 4 * n:4 * n + 4, :].rearrange("p a b -> p (a b)"), src, ACT.Copy).then_inc(s_te, 1)
                else:
                    m = 4 * (n - 8)
                    nc.scalar.activation(dnT[:, m:m + 4, :].rearrange("p a b -> p (a b)"), src, ACT.Copy, scale=0.5).then_inc(s_te, 1)

            def qkv(b, ph):
                f = 0 if ph == "g" else 1
                for h in range(2):
                    act.wait_ge(s_xtp, b * 4 + 2 * f + h + 1)
                    if ph == "g" and h == 0:
                        act.wait_ge(s_u, 1 + b * FU)
                    nc.scalar.activation(xT[ph][:, h * 512:(h + 1) * 512], SP_[:, h * 512:(h + 1) * 512], ACT.Copy).then_inc(s_xts, 1)
                if ph == "g":
                    act.wait_ge(s_lx, b + 1)
                    nc.scalar.activation(cw[:, :, :], lg[:, :, :], ACT.Exp).then_inc(s_le, 1)
                act.wait_ge(s_rot, b * 2 + f + 1)
                nc.scalar.activation(rtmp[:, :, :], rot[:, :, :], ACT.Square).then_inc(s_sq, 1)
                for h in range(4):
                    act.wait_ge(s_qkt, b * 10 + 5 * f + h + 1)
                    nc.scalar.activation(qT[:, 2 * h:2 * h + 2, :].rearrange("p a b -> p (a b)"),
                                         SP_[:, h * 512:(h + 1) * 512].bitcast(fp16), ACT.Copy).then_inc(s_qTs, 1)

            def exps(b, units):
                for job in [j for j in JOBS if j[0] in units]:
                    u, part = job
                    ph, t, kt = UNITS[u]
                    act.wait_ge(s_sc, b * NJ + JOB[job] + 1)
                    if part == 0 and u >= 3:
                        act.wait_ge(s_pv, b * NU + u - 2)
                    if part < 2:
                        nc.scalar.activation(P[:, u % 3, part * 1024:(part + 1) * 1024], pair_of(job), ACT.Exp,
                                             scale=EXP_SCALE).then_inc(s_ex, 1)
                    else:
                        nc.scalar.activation(Pp[128 - WIN:128, t % 2, :], pair_of(job)[128 - WIN:128, 0:512], ACT.Exp,
                                             scale=EXP_SCALE).then_inc(s_ex, 1)

            with act.Fori(0, B) as b:
                qkv(b, "g")
                exps(b, range(0, len(G_UNITS)))
                qkv(b, "l")
                exps(b, range(len(G_UNITS), NU))
                for n in range(FU):
                    ch, e = divmod(n, E)
                    act.wait_ge(s_u, 1 + b * FU + n + 1)
                    if n >= 2:
                        act.wait_ge(s_aw, 1 + b * FU + n - 1)
                    for i in range(IT):
                        last = nc.scalar.activation(up[:, n % 2, i * CH:(i + 1) * CH], OP[:, i * CH:(i + 1) * CH], ACT.Identity,
                                                    bias=gub[:, e, IT + i:IT + i + 1])
                    last.then_inc(s_us, 1)
                    act.wait_ge(s_gs, 1 + b * FU + n + 1)
                    nc.scalar.activation(sig[:, n % 2, :], gate[:, n % 2, :], ACT.Tanh, scale=ALPHA / 2).then_inc(s_th, 1)
                    if n % E == 3 and n >= E:
                        act.wait_ge(s_yt, b * NCH + n // E)
                        nc.scalar.activation(yth, (M0, M1)[n // E - 1], ACT.Tanh, scale=0.5).then_inc(s_yth, 1)
                act.wait_ge(s_yt, b * NCH + NCH)
                act.wait_ge(s_out, 1 + b * NCH + NCH - 1)
                nc.scalar.activation(yth, (M0, M1)[NCH - 1], ACT.Tanh, scale=0.5).then_inc(s_yth, 1)

        @block.gpsimd
        def _(pool):
            nc.gpsimd.memset(kz[:, :, :], 0.0).then_inc(s_zero, 1)
            nc.gpsimd.memset(v[:, :, :, :], 0.0).then_inc(s_plink, 1)
            nc.gpsimd.memset(Pp[:, :, :], 0.0).then_inc(s_zero, 1)
            pool.wait_ge(s_plink, 1)
            nc.gpsimd.memset(v[:, :, :, HD:HD + 1], 1.0).then_inc(s_zero, 1)

            def qkv(b, ph):
                f = 0 if ph == "g" else 1
                pool.wait_ge(s_pev, b * 8 + 4 * f + 4)
                cos = rope[ph][:, 0:T * HD].rearrange("p (t o d) -> p t o d", t=T, o=1).to_broadcast([128, T, HEADS, HD])
                nc.gpsimd.tensor_tensor(rot[:, :, :].rearrange("p (t h) d -> p t h d", t=T), qk[:, :, :].rearrange("p (t h) d -> p t h d", t=T),
                                        cos, ALU.mult).then_inc(s_cos, 1)

            def masks(b, units):
                for job in [j for j in MASKJOBS if j[0] in units]:
                    u, part = job
                    ph, t, kt = UNITS[u]
                    pool.wait_ge(s_ex, b * NJ + JOB[job] + 1)
                    if ph == "l":
                        pool.wait_ge(s_mk, b * len(MJ) + MJ[job])
                    pool.sem_inc(s_pass["pool"], 1)
                    if part < 2:
                        p = P[:, u % 3, part * 1024:(part + 1) * 1024].rearrange("p (h q) -> p h q", q=128)
                        causal = nc.gpsimd.affine_select(out=p, in_=p, compare_op=ALU.is_ge, fill=0.0, base=0,
                                                         pattern=[[0, 8], [1, 128]], channel_multiplier=-1)
                        if ph == "g":
                            causal.then_inc(s_mk, 1)
                        else:
                            causal.then_inc(s_plink, 1)
                            pool.wait_ge(s_plink, b * 2 * T + 2 * t + part + 2)
                            pool.sem_inc(s_pass["pool"], 1)
                            nc.gpsimd.affine_select(out=p, in_=p, compare_op=ALU.is_ge, fill=0.0, base=WIN - 1,
                                                    pattern=[[0, 8], [-1, 128]], channel_multiplier=1).then_inc(s_mk, 1)
                    else:
                        p = Pp[128 - WIN:128, t % 2, :].rearrange("p (h q) -> p h q", q=WIN)
                        nc.gpsimd.affine_select(out=p, in_=p, compare_op=ALU.is_ge, fill=0.0, base=-1,
                                                pattern=[[0, H], [-1, WIN]], channel_multiplier=1).then_inc(s_mk, 1)

            with pool.Fori(0, B) as b:
                qkv(b, "g")
                masks(b, range(0, len(G_UNITS)))
                qkv(b, "l")
                masks(b, range(len(G_UNITS), NU))
                pool.wait_ge(s_wb, b * 16 + 16)
                for n in range(FU):
                    ch, e = divmod(n, E)
                    pool.wait_ge(s_us, 1 + b * FU + n + 1)
                    pool.sem_inc(s_pass["pool"], 1)
                    nc.gpsimd.tensor_scalar(up[:, n % 2, :], up[:, n % 2, :], 1.0 + LIMIT, 1.0 - LIMIT, ALU.min, ALU.max).then_inc(s_uc, 1)
                    pool.wait_ge(s_a, b * FU + n + 1)
                    if n >= 2:
                        pool.wait_ge(s_dn, 1 + b * (FU + NCH) + n - 1 + (n - 2) // E)
                    w = wb[:, e * S + ch * CH:e * S + (ch + 1) * CH].rearrange("p (o c) -> p o c", o=1).to_broadcast([128, IT, CH])
                    nc.gpsimd.tensor_tensor(aw[:, n % 2, :].rearrange("p (i c) -> p i c", i=IT),
                                            up[:, n % 2, :].rearrange("p (i c) -> p i c", i=IT), w, ALU.mult).then_inc(s_aw, 1)

        @block.vector
        def _(dve):
            steps = [0, 0, None]

            def link(ins):
                ins.then_inc(s_link, 1)
                if steps[2] is None:
                    steps[0] += 1
                    dve.wait_ge(s_link, steps[0])
                else:
                    steps[1] += 1
                    dve.wait_ge(s_link, steps[2] * VSTEPS + steps[0] + steps[1])

            def rsqrt(y, x, n):
                t0, t1 = ntmp[:, 0, 0:n], ntmp[:, 1, 0:n]
                link(nc.vector.tensor_scalar(y.bitcast(i32), x.bitcast(i32), -0.5, MAGIC, ALU.mult, ALU.add))
                for _ in range(3):
                    link(nc.vector.scalar_tensor_tensor(t0, y, -0.5, y, ALU.mult, ALU.mult))
                    link(nc.vector.tensor_tensor(t1, t0, x, ALU.mult))
                    link(nc.vector.scalar_tensor_tensor(y, t1, 1.5, y, ALU.add, ALU.mult))

            dve.wait_ge(s_att, 13 * 16)
            for ph in ("g", "l"):
                nc.vector.tensor_scalar(wproj[ph][:, 0:H * HD].rearrange("p (j c d) -> p j c d", j=J, c=KVH),
                                        wq_in[ph][:, :].rearrange("p (c j d) -> p j c d", j=J, c=KVH), norm_w[ph][:, 0:1], None, ALU.mult)
            nc.vector.tensor_scalar(wproj["l"][:, H * HD:PROJ], wkv_in[:, :], norm_w["l"][:, 0:1], None, ALU.mult)
            dve.wait_ge(s_pw, 1)
            nc.vector.tensor_copy(kvdT[:, :], M0[0:32, 0:128]).then_inc(s_pe_, 1)
            dve.wait_ge(s_pw, 2)
            nc.vector.tensor_scalar(wproj["g"][:, H * HD:PROJ], M0[:, 128:192], norm_w["g"][:, 0:1], None, ALU.mult).then_inc(s_pe_, 1)
            dve.wait_ge(s_pw, 3)
            nc.vector.tensor_copy(rwT[:, :], M1[:, 0:E]).then_inc(s_pe_, 1)
            bT = M1[:, 64:64 + 4 * E].rearrange("p (e m) -> p e m", m=4)
            nc.vector.tensor_copy(gub[:, :, 0:IT], bT[:, :, 0:IT]).then_inc(s_pe_, 1)
            nc.vector.tensor_scalar(gub[:, :, IT:2 * IT], bT[:, :, IT:2 * IT], 1.0, None, ALU.add).then_inc(s_pe_, 1)
            dve.wait_ge(s_zero, 3)

            def bcast(ap, n):
                m = ap.shape[1]
                return ap.rearrange("p (m o) -> p m o", o=1).to_broadcast([128, m, n])

            def layernorm(b):
                dve.wait_ge(s_x, b * 16 + 16)
                for t in range(T):
                    last = nc.vector.bn_stats(stats[:, t, :], xs[:, t, :])
                link(last)
                dve.sem_inc(s_pass["dve"], 1)
                for t in range(T):
                    last = nc.vector.bn_aggr(mv[:, t, :], stats[:, t, :])
                link(last)
                link(nc.vector.tensor_scalar(rs[:, 2, :], mv[:, :, 1], LN_EPS, None, ALU.add))
                rsqrt(rs[:, 0, :], rs[:, 2, :], T)
                link(nc.vector.tensor_tensor(rs[:, 3, :], rs[:, 0, :], rs[:, 0, :], ALU.mult))
                link(nc.vector.tensor_tensor(rs[:, 3, :], rs[:, 3, :], mv[:, :, 1], ALU.mult))
                link(nc.vector.tensor_scalar(rs[:, 3, :], rs[:, 3, :], RMS_EPS, None, ALU.add))
                rsqrt(rs[:, 1, :], rs[:, 3, :], T)
                for t in range(T):
                    last = nc.vector.tensor_scalar(xn[:, t, :], xs[:, t, :], mv[:, t, 0:1], rs[:, 0, t:t + 1], ALU.subtract, ALU.mult)
                last.then_inc(s_xn, 1)

            def rms(b):
                sq = rtmp[:, 0:T * 16, :].rearrange("p (t a) d -> p t (a d)", t=T)
                link(nc.vector.tensor_tensor(sq, x1[:, :, :], x1[:, :, :], ALU.mult))
                link(nc.vector.tensor_reduce(rs[:, 2, :], sq, AXX, ALU.add))
                link(nc.vector.tensor_scalar(rs[:, 3, :], rs[:, 2, :], 1.0 / D, RMS_EPS, ALU.mult, ALU.add))
                rsqrt(rs[:, 1, :], rs[:, 3, :], T)

            def router(b):
                dve.wait_ge(s_lg, b + 1)
                rbb = rb[:, :].rearrange("p (o e) -> p o e", o=1).to_broadcast([128, T, E])
                link(nc.vector.tensor_tensor(lg[:, :, :], OP[:, 0:T * E].rearrange("p (t e) -> p t e", e=E), rbb, ALU.add))
                flat = lg[:, :, :].rearrange("p t e -> p (t e)")
                mine = bcast(flat, E).rearrange("p (t e) f -> p t e f", t=T)
                other = lg[:, :, :].rearrange("p t (o e) -> p t o e", o=1).to_broadcast([128, T, E, E])
                p4 = [pair[:, i, :].rearrange("p (t e f) -> p t e f", t=T, e=E) for i in range(2)]
                nc.vector.tensor_tensor(p4[0], other, mine, ALU.is_gt)
                link(nc.vector.tensor_tensor(p4[1], other, mine, ALU.is_equal))
                before = earlier.rearrange("p (o e) -> p o e", o=1).to_broadcast([128, T, E * E])
                flat1 = pair[:, 1, :].rearrange("p (t e) -> p t e", t=T)
                link(nc.vector.tensor_tensor(flat1, flat1, before, ALU.mult))
                link(nc.vector.tensor_tensor(pair[:, 0, :], pair[:, 0, :], pair[:, 1, :], ALU.add))
                link(nc.vector.tensor_reduce(rank[:, :], pair[:, 0, :].rearrange("p (a f) -> p a f", f=E), AXX, ALU.add))
                link(nc.vector.tensor_reduce(mx[:, 0, :], lg[:, :, :], AXX, ALU.max))
                nc.vector.tensor_tensor(lg[:, :, :], lg[:, :, :], bcast(mx[:, 0, :], E), ALU.subtract).then_inc(s_lx, 1)
                dve.wait_ge(s_le, b + 1)
                cwf = cw[:, :, :].rearrange("p t e -> p (t e)")
                link(nc.vector.scalar_tensor_tensor(cwf, rank[:, :], TOPK - 0.5, cwf, ALU.is_lt, ALU.mult))
                link(nc.vector.tensor_reduce(mx[:, 0, :], cw[:, :, :], AXX, ALU.add))
                link(nc.vector.reciprocal(mx[:, 1, :], mx[:, 0, :]))
                nc.vector.tensor_tensor(cw[:, :, :], cw[:, :, :], bcast(mx[:, 1, :], E), ALU.mult).then_inc(s_cw, 1)
                dve.wait_ge(s_wtp, b + 1)
                dve.wait_ge(s_dn, 1 + b * (FU + NCH))
                dve.wait_ge(s_wst, 16 + b * 16)
                nc.vector.tensor_copy(wT[:, :], OP[0:E, :]).then_inc(s_wts, 1)

            def qkv(b, ph):
                f = 0 if ph == "g" else 1
                banks = [SP_[:, 1024:1536], SP_[:, 1536:2048], M0, M1]
                for h in range(4):
                    dve.wait_ge(s_prj, b * 8 + 4 * f + h + 1)
                    src = banks[h][:, 0:2 * PROJ].rearrange("p (t n) -> p t n", t=2)
                    r = rs[:, 1, 2 * h:2 * h + 2]
                    nc.vector.tensor_tensor(qk[:, 2 * h * HEADS:(2 * h + 2) * HEADS, :].rearrange("p (t a) d -> p t (a d)", t=2),
                                            src[:, :, 0:QK], bcast(r, QK), ALU.mult)
                    nc.vector.tensor_tensor(v[:, 2 * h:2 * h + 2, :, 0:HD], src[:, :, QK:PROJ].rearrange("p t (c d) -> p t c d", c=KVH),
                                            r.rearrange("p (t o q) -> p t o q", o=1, q=1).to_broadcast([128, 2, KVH, HD]), ALU.mult) \
                        .then_inc(s_pev, 1)
                if ph == "g":
                    router(b)
                dve.wait_ge(s_pev, b * 8 + 4 * f + 4)
                sin = rope[ph][:, T * HD:2 * T * HD].rearrange("p (t o d w) -> p t o d w", t=T, o=1, w=2)
                q5 = qk[:, :, :].rearrange("p (t h) (d w) -> p t h d w", t=T, w=2)
                r5 = rtmp[:, :, :].rearrange("p (t h) (d w) -> p t h d w", t=T, w=2)
                nc.vector.tensor_tensor(r5[:, :, :, :, 0], q5[:, :, :, :, 1], sin[:, :, :, :, 0].to_broadcast([128, T, HEADS, HD // 2]), ALU.mult)
                link(nc.vector.tensor_tensor(r5[:, :, :, :, 1], q5[:, :, :, :, 0], sin[:, :, :, :, 1].to_broadcast([128, T, HEADS, HD // 2]), ALU.mult))
                dve.wait_ge(s_cos, b * 2 + f + 1)
                flat = lambda a: a[:, :, :].rearrange("p a d -> p (a d)")
                nc.vector.tensor_tensor(flat(rot), flat(rot), flat(rtmp), ALU.add).then_inc(s_rot, 1)
                dve.wait_ge(s_sq, b * 2 + f + 1)
                link(nc.vector.tensor_reduce(msq[:, :], rtmp[:, :, :], AXX, ALU.add))
                c = 1.0 / (QKSCALE * QKSCALE)
                link(nc.vector.tensor_scalar(msq[:, :], msq[:, :], c / HD, c * RMS_EPS, ALU.mult, ALU.add))
                rsqrt(rn[:, :], msq[:, :], T * HEADS)
                link(nc.vector.tensor_tensor(rot[:, :, :], rot[:, :, :], bcast(rn[:, :], HD), ALU.mult))
                link(nc.vector.tensor_copy(stk[:, :, 0, :], rot[:, :, :]))
                link(nc.vector.tensor_tensor(stk[:, :, 3, :], rot[:, :, :], stk[:, :, 0, :], ALU.subtract))
                st = stk[:, :, :, :].rearrange("p (t h) w d -> p t h w d", t=T)
                nc.vector.tensor_copy(st[:, :, 0:H, 1, :], st[:, :, 0:H, 0, :])
                nc.vector.tensor_copy(st[:, :, 0:H, 2, :], st[:, :, 0:H, 3, :])
                nc.vector.tensor_copy(st[:, :, H:HEADS, 1, :], st[:, :, H:HEADS, 3, :])
                link(nc.vector.tensor_copy(st[:, :, H:HEADS, 2, :], st[:, :, H:HEADS, 0, :]))
                nc.vector.tensor_copy(ntmp[:, 0, 0:1], ntmp[:, 1, 0:1]).then_inc(s_stk, 1)
                dve.wait_ge(s_qkt, b * 10 + 5 * f + 5)
                for c in range(KVH):
                    last = nc.vector.tensor_copy(kz[32 * c:32 * c + 32, c, :], M0.bitcast(fp16)[32 * c:32 * c + 32, :])
                last.then_inc(s_kTs, 1)

            def post(b, units):
                first, end = units[0], units[-1] + 1
                for u in range(first, end + 4):
                    if u - 2 in POST and first <= u - 2 < end:
                        p = POST[u - 2]
                        dve.wait_ge(s_ot, b * NP + p + 1)
                        o = M0.rearrange("p (j c d) -> p j c d", j=J, c=KVH)
                        r = rec[:, p % 2, :].rearrange("p (j c) -> p j c", j=J)
                        link(nc.vector.reciprocal(r, o[:, :, :, HD]))
                        nc.vector.tensor_tensor(on[:, p % 2, :].rearrange("p (c j d) -> p j c d", c=KVH, j=J), o[:, :, :, 0:HD],
                                                rec[:, p % 2, :].rearrange("p (j c o) -> p j c o", j=J, o=1).to_broadcast([128, J, KVH, HD]),
                                                ALU.mult).then_inc(s_on, 1)
                    if u - 3 in POST and first <= u - 3 < end:
                        p = POST[u - 3]
                        dve.wait_ge(s_ont, b * NP + p + 1)
                        nc.vector.tensor_copy(onT[:, p % 2, :], M1[:, 0:128]).then_inc(s_ons, 1)
                    if u - 4 in POST and first <= u - 4 < end:
                        p = POST[u - 4]
                        ph, t, _ = UNITS[u - 4]
                        dve.wait_ge(s_wo, b * NP + p + 1)
                        src, dst = (xn, x1) if ph == "g" else (x1, ss)
                        nc.vector.tensor_tensor(dst[:, t, :], M1[:, 128:256], src[:, t, :], ALU.add).then_inc(s_x1, 1)
                    if u - 1 in POST and first <= u - 1 < end:
                        p = POST[u - 1]
                        dve.wait_ge(s_pv, b * NU + u)
                        nc.vector.tensor_copy(oT[:, p % 2, :], OP[:, (p % 2) * 512:(p % 2 + 1) * 512]).then_inc(s_o, 1)
                dve.wait_ge(s_x1, b * NP + (T if units[0] == 0 else NP))

            def ffn(b):
                def gates(n):
                    e = n % E
                    dve.wait_ge(s_g, b * FU + n + 1)
                    if n >= 2:
                        dve.wait_ge(s_a, b * FU + n - 1)
                    for i in range(IT):
                        last = nc.vector.tensor_scalar(gate[:, n % 2, i * CH:(i + 1) * CH], SP_[:, (n % 2) * 1024 + i * CH:(n % 2) * 1024 + (i + 1) * CH],
                                                       gub[:, e, i:i + 1], LIMIT, ALU.add, ALU.min)
                    last.then_inc(s_gs, 1)

                gates(0)
                for n in range(FU):
                    if n + 1 < FU:
                        gates(n + 1)
                    dve.wait_ge(s_th, b * FU + n + 1)
                    link(nc.vector.scalar_tensor_tensor(sig[:, n % 2, :], sig[:, n % 2, :], 1.0, gate[:, n % 2, :], ALU.add, ALU.mult))
                    dve.wait_ge(s_uc, b * FU + n + 1)
                    nc.vector.tensor_tensor(up[:, n % 2, :], up[:, n % 2, :], sig[:, n % 2, :], ALU.mult).then_inc(s_a, 1)
                    if n % E == 1 and n >= E:
                        evac(b, n // E - 1)
                    if n % E == 4 and n >= E:
                        combine(b, n // E - 1)
                evac(b, NCH - 1)
                combine(b, NCH - 1)

            def evac(b, ch):
                dve.wait_ge(s_dn, 1 + b * (FU + NCH) + (ch + 1) * (E + 1))
                nc.vector.tensor_copy(yT, (M0, M1)[ch]).then_inc(s_ys, 1)

            def combine(b, ch):
                ts = slice(ch * CH // 128, (ch + 1) * CH // 128)
                flat = lambda a: a[:, ts, :].rearrange("p t d -> p (t d)")
                dve.wait_ge(s_yth, b * NCH + ch + 1)
                if ch == 0:
                    dve.wait_ge(s_st, 16 + b * NCH * 16)
                link(nc.vector.scalar_tensor_tensor(yth, yth, 1.0, (M0, M1)[ch], ALU.add, ALU.mult))
                link(nc.vector.scalar_tensor_tensor(yth, yth, 0.5, flat(ss), ALU.mult, ALU.mult))
                nc.vector.tensor_tensor(flat(ys), yth, flat(xs), ALU.add).then_inc(s_out, 1)

            with dve.Fori(0, B) as b:
                steps[2] = b
                layernorm(b)
                qkv(b, "g")
                post(b, range(0, len(G_UNITS)))
                rms(b)
                qkv(b, "l")
                post(b, range(len(G_UNITS), NU))
                ffn(b)
            assert steps[1] == VSTEPS, steps


VSTEPS = 118

_INS = ["L0_attn_hidden", "L0_attn_norm1_w", "L0_attn_norm2_w", "L0_attn_g_wq", "L0_attn_g_kv_down", "L0_attn_g_k_up",
        "L0_attn_g_v_up", "L0_attn_g_wo", "L0_attn_l_wq", "L0_attn_l_wk", "L0_attn_l_wv", "L0_attn_l_wo",
        "L0_ffn_router_weight", "L0_ffn_router_bias", "L0_ffn_gate_up_proj", "L0_ffn_gate_up_proj_bias",
        "L0_ffn_down_proj", "L0_ffn_down_proj_bias"]


def _constants():
    import numpy as np
    f = np.float32
    parts = [np.eye(128, dtype=f), np.tile(np.tril(np.ones((E, E), f), -1).reshape(1, -1), (128, 1))]
    for base in (1000000.0, 10000.0):
        inv = (f(1.0) / f(base) ** (np.arange(0, HD, 2, dtype=f) / f(HD))).astype(f)
        ang = np.arange(S, dtype=f)[:, None] * inv[None, :]
        cos, sin = np.cos(ang), np.sin(ang)
        for a in (np.stack([cos, cos], -1), np.stack([-sin, sin], -1)):
            parts.append(a.reshape(T, 128, HD).transpose(1, 0, 2).reshape(128, T * HD).astype(f))
    return np.ascontiguousarray(np.concatenate(parts, 1)), np.eye(128, dtype=np.float16)


def kernel(**inputs):
    import numpy as _np
    import concourse.bacc as _bacc
    from concourse import mybir as _mybir
    from concourse.bass_utils import run_bass_kernel_spmd as _run

    nc = _bacc.Bacc("TRN2", target_bir_lowering=False, num_devices=1)
    arrays, args = {}, []
    c32, c16 = _constants()
    for name, a in [(n, _np.ascontiguousarray(inputs[n])) for n in _INS] + [("const32", c32), ("const16", c16)]:
        arrays[f"in_{name}_dram"] = a
        args.append(nc.dram_tensor(f"in_{name}_dram", a.shape, _mybir.dt.from_np(a.dtype), kind="ExternalInput").ap())
    args.append(nc.dram_tensor("out_0_dram", (B, S, D), _mybir.dt.float32, kind="ExternalOutput").ap())
    gated_attention_moe_kernel(nc, *args)
    r = _run(nc, [arrays], core_ids=[0])
    return r.results[0]["out_0_dram"]
```

```python
import concourse.bass as bass
from concourse import mybir
from contextlib import ExitStack

B, S, D = 2, 1024, 128
T = S // 128
H, KVH, HD = 16, 4, 8
J = H // KVH
WIN = 32
E, I = 8, 256
TOPK = 4
LIMIT, ALPHA = 7.0, 1.702
LN_EPS, RMS_EPS = 1e-5, 1e-6
HEADS = H + KVH
QK = HEADS * HD
PROJ = QK + KVH * HD
PARTS = 4
QKSCALE = 64.0
EXP_SCALE = 1.0 / (QKSCALE * QKSCALE * HD ** 0.5)
MAGIC = float(0x5F3759DF)
CH = 512
NCH = S // CH
IT = I // 128
WSCALE = 32.0
ACC = WSCALE * WSCALE
HU = NCH * E * IT
G_UNITS = [(t, kt) for t in range(T) for kt in [t] + list(range(t))]
NG = len(G_UNITS)
ENDS = {u: G_UNITS[u][0] for u in range(NG) if u + 1 == NG or G_UNITS[u + 1][0] != G_UNITS[u][0]}
NP = 2 * T
LJ = 5 * T - 1
NQ, NR = 10, 4
NW = 12
Q0 = 3


def local_job(t, k):
    return 5 * t + k - (1 if t > 0 else 0)


def schedule():
    def spread(others, fills):
        out, at = [], 0
        for i, f in enumerate(fills):
            to = (i + 1) * len(others) // len(fills)
            out += [f] + others[at:to]
            at = to
        return out

    steps = []
    for k in range(max(NQ, NW)):
        steps += [("Q", 0, "g", k)] * (k < NQ) + [("W", 0, k)] * (k < NW)
    steps += [("R", 0, k) for k in range(NR - 1)]
    for b in range(B):
        steps += [("R", b, NR - 1)]
        steps += [("G", b, u) for u in range(-1, NG + 4)]
        others = [("Q", b, "l", k) for k in range(Q0 - 1, NQ)]
        others += [("L", b, t, k) for t in range(T + 2) for k in range(3) if (t, k) < (T + 1, 1)]
        if b + 1 < B:
            others += [("Q", b + 1, "g", k) for k in range(NQ)] + [("R", b + 1, k) for k in range(NR - 1)]
        fills = []
        for n in range(HU + 2):
            fills.append(("F", b, n))
            if n >= 2 and (n - 2) % (E * IT) == E * IT - 1:
                fills.append(("Y", b, (n - 2) // (E * IT)))
        steps += spread(others, fills)
        steps += [("O", b, c) for c in range(NCH)]
    return steps


def gated_attention_moe_kernel(nc, hidden, n1, n2, g_wq, g_kvd, g_ku, g_vu, g_wo, l_wq, l_wk, l_wv, l_wo,
                               r_w, r_b, gu_w, gu_b, dn_w, dn_b, c32, c16, out):
    fp32, fp16, i32 = mybir.dt.float32, mybir.dt.float16, mybir.dt.int32
    ALU = mybir.AluOpType
    ACT = mybir.ActivationFunctionType
    AXX = mybir.AxisListType.X
    SCHEDULE = schedule()

    ctx = ExitStack()
    with ctx:
        def sb(name, shape, dt=fp32):
            return ctx.enter_context(nc.sbuf_tensor(name, shape, dt))

        def sem(name):
            return ctx.enter_context(nc.semaphore(name))

        k32 = sb("k32", [128, c32.shape[1]])
        ident = k32[:, 0:128]
        earlier = k32[:, 128:192]
        rope = {"g": k32[:, 192:320], "l": k32[:, 320:448]}
        k16 = sb("k16", [128, 128], fp16)
        wq_in = {"g": sb("wq_g", [128, H * HD]), "l": sb("wq_l", [128, H * HD])}
        wkv_in = sb("wkv_in", [128, 2 * KVH * HD])
        kvd = sb("kvd", [128, 32])
        kvdT = sb("kvdT", [32, 128])
        kvu = sb("kvu", [32, 2 * KVH * HD])
        norm_w = {"g": sb("n1w", [128, 1]), "l": sb("n2w", [128, 1])}
        wproj = {"g": sb("wproj_g", [128, PROJ]), "l": sb("wproj_l", [128, PROJ])}
        wo = {"g": sb("wo_g", [128, D]), "l": sb("wo_l", [128, D])}
        rw_in = sb("rw_in", [E, D])
        rwT = sb("rwT", [128, E])
        rb = sb("rb", [128, E])
        gub_in = sb("gub_in", [4 * E, 128])
        gub = sb("gub", [128, E, 2 * IT])
        guh = sb("guh", [128, 4 * E, 128], fp16)
        gul = sb("gul", [128, 4 * E, 128], fp16)
        dnT = sb("dnT", [128, 2 * E, D])
        dnb = sb("dnb", [E, D])

        xs = sb("xs", [128, B, T, D])
        xn = sb("xn", [128, T, D])
        x1 = sb("x1", [128, T, D])
        ss = sb("ss", [128, T, D])
        xT = sb("xT", [128, S])
        xh = sb("xh", [128, S], fp16)
        xl = sb("xl", [128, S], fp16)
        stats = sb("stats", [128, T, 6])
        mv = sb("mv", [128, T, 2])
        rs = sb("rs", [128, 4, T])
        ntmp = sb("ntmp", [128, 2, T * HEADS])
        qk = sb("qk", [128, T * HEADS, HD])
        rot = sb("rot", [128, T * HEADS, HD])
        rtmp = sb("rtmp", [128, T * HEADS, HD])
        msq = sb("msq", [128, T * HEADS])
        rn = sb("rn", [128, T * HEADS])
        stk = sb("stk", [128, T * HEADS, PARTS, HD], fp16)
        qT = sb("qT", [128, T, J * 128], fp16)
        kz = sb("kz", [128, KVH, S], fp16)
        v = sb("v", [128, T, KVH, 32])
        P = sb("P", [128, 3, 4 * 512])
        Pp = sb("Pp", [128, 2, 512])
        oT = sb("oT", [128, 2, 512])
        on = sb("on", [128, 2, 128])
        onT = sb("onT", [128, 2, 128])
        rec = sb("rec", [128, 2, H])
        lg = sb("lg", [128, T, E])
        rank = sb("rank", [128, T * E])
        cw = sb("cw", [128, T, E])
        mx = sb("mx", [128, 2, T])
        wT = sb("wT", [E, S])
        wb = sb("wb", [128, E * S])
        gate = sb("gate", [128, 2, CH])
        sig = sb("sig", [128, 2, CH])
        up = sb("up", [128, 2, CH])
        aw = sb("aw", [128, 2, CH])
        yT = sb("yT", [128, CH])
        ys = sb("ys", [128, T, D])
        gu_in = wb[:, 0:4096].rearrange("p (m d) -> p m d", d=128)
        dn_in = wb[:, 4096:6144].rearrange("p (e i) -> p e i", i=I)

        ps = ctx.enter_context(nc.psum_tensor("ps", [128, 4096], fp32))

        def bank(i, n=1):
            return ps[:, i * 512:(i + n) * 512]

        PAIR = [bank(0, 2), bank(4, 2)]
        OB = [bank(2), bank(6)]
        MA, MB = bank(3), bank(7)
        LS = [bank(0), bank(1)]
        LO, LM = bank(2), bank(3)
        RING = [bank(4), bank(5), bank(6)]
        Y = bank(7)
        PRJ = [bank(2), bank(3), bank(0), bank(1)]
        KT, QT = bank(0), [bank(1), bank(2), bank(3), bank(0)]

        w_dram = nc.dram_tensor("combine_rows", [B, E, S], fp32, kind="Internal").ap()

        s_att = sem("attn_inputs_loaded")
        s_ffn = sem("ffn_inputs_loaded")
        s_zero = sem("pads_written")
        s_pw = sem("prep_product")
        s_pe_ = sem("prep_evacuated")
        s_tp = sem("ffn_weight_transposed")
        s_te = sem("ffn_weight_hi_written")
        s_tl = sem("ffn_weight_lo_written")
        s_x = [sem(f"x_loaded_{b}") for b in range(B)]
        s_link = sem("vector_step")
        s_plink = sem("pool_step")
        s_xn = sem("normed")
        s_xtp = sem("x_transposed")
        s_xts = sem("xT_written")
        s_xh = sem("x_hi_written")
        s_xl = sem("x_lo_written")
        s_prj = sem("projected")
        s_pev = sem("projection_evacuated")
        s_cos = sem("rope_cos_done")
        s_rot = sem("rotated")
        s_sq = sem("squares_done")
        s_stk = sem("parts_stacked")
        s_kt = sem("k_transposed")
        s_qt = sem("q_transposed")
        s_qTs = sem("qT_written")
        s_kTs = sem("kT_written")
        s_lg = sem("logits_done")
        s_lx = sem("logits_shifted")
        s_le = sem("logits_exp")
        s_cw = sem("combine_done")
        s_wtp = sem("combine_transposed")
        s_wts = sem("wT_written")
        s_wst = sem("combine_stored")
        s_wb = sem("combine_broadcast")
        s_sc = sem("scores_done")
        s_ex = sem("exp_done")
        s_mk = sem("masked")
        s_pv = sem("pv_done")
        s_lsc = sem("local_scores_done")
        s_lex = sem("local_exp_done")
        s_lmk = sem("local_masked")
        s_lpv = sem("local_pv_done")
        s_o = sem("o_evacuated")
        s_ot = sem("o_transposed")
        s_on = sem("o_normalised")
        s_ont = sem("on_transposed")
        s_ons = sem("onT_written")
        s_wo = sem("wo_done")
        s_x1 = sem("residual_added")
        s_g = sem("gate_done")
        s_u = sem("up_done")
        s_gs = sem("gate_evacuated")
        s_th = sem("tanh_done")
        s_us = sem("up_evacuated")
        s_a = sem("act_done")
        s_aw = sem("act_weighted")
        s_dn = sem("down_done")
        s_y = sem("y_done")
        s_ys = sem("y_evacuated")
        s_yt = sem("y_transposed")
        s_yth = sem("y_tanh")
        s_yd = sem("y_times_tanh")
        s_out = sem("result_ready")
        s_st = sem("result_stored")

        block = ctx.enter_context(nc.Block())

        @block.sync
        def _(sp):
            def load_x(b):
                sp.dma_start(xs[:, b, :, :], hidden[b, :, :].rearrange("(t p) d -> p t d", p=128)).then_inc(s_x[b], 16)

            load_x(0)
            for dst, src in ((k32[:, :], c32), (wq_in["g"][:, :], g_wq), (kvd[:, :], g_kvd),
                             (kvu[:, 0:32], g_ku), (kvu[:, 32:64], g_vu), (norm_w["g"][:, :], n1.rearrange("(p o) -> p o", o=1)),
                             (norm_w["l"][:, :], n2.rearrange("(p o) -> p o", o=1)), (k16[:, :], c16), (wo["g"][:, :], g_wo),
                             (wq_in["l"][:, :], l_wq), (wkv_in[:, 0:32], l_wk), (wkv_in[:, 32:64], l_wv), (wo["l"][:, :], l_wo)):
                sp.dma_start(dst, src).then_inc(s_att, 16)
            for dst, src in ((rw_in[:, :], r_w), (rb[:, :], r_b.rearrange("(o e) -> o e", o=1).to_broadcast([128, E])),
                             (gub_in[:, :], gu_b.rearrange("e (m j) -> (e m) j", j=128)), (dnb[:, :], dn_b),
                             (gu_in, gu_w.rearrange("e (m j) d -> j (e m) d", j=128)),
                             (dn_in, dn_w.rearrange("e d i -> d e i"))):
                sp.dma_start(dst, src).then_inc(s_ffn, 16)
            for b in range(1, B):
                load_x(b)
            for b in range(B):
                sp.wait_ge(s_wts, b + 1)
                sp.dma_start(w_dram[b, :, :], wT[:, :]).then_inc(s_wst, 16)
                sp.wait_ge(s_wst, 16 * (b + 1))
                if b > 0:
                    sp.wait_ge(s_aw, b * HU)
                else:
                    sp.wait_ge(s_te, 12)
                    sp.wait_ge(s_tl, 8)
                sp.dma_start(wb[:, :], w_dram[b, :, :].rearrange("(o e) s -> o (e s)", o=1)
                             .to_broadcast([128, E * S])).then_inc(s_wb, 16)
                for c in range(NCH):
                    sp.wait_ge(s_out, b * NCH + c + 1)
                    sp.dma_start(out[b, c * CH:(c + 1) * CH, :].rearrange("(t p) d -> p t d", p=128),
                                 ys[:, c * CH // 128:(c + 1) * CH // 128, :]).then_inc(s_st, 16)
            sp.wait_ge(s_st, B * NCH * 16)

        @block.tensor
        def _(pe):
            pe.wait_ge(s_att, 13 * 16)
            nc.tensor.transpose(MB[0:32, 0:128], kvd[:, :], ident).then_inc(s_pw, 1)
            pe.wait_ge(s_pe_, 1)
            nc.tensor.matmul(MB[:, 128:192], kvdT[:, :], kvu[:, :], start=True, stop=True).then_inc(s_pw, 1)

            def weights(b, n):
                if n == 0:
                    pe.wait_ge(s_ffn, 6 * 16)
                    pe.wait_ge(s_pe_, 2)
                    nc.tensor.transpose(MB[:, 0:E], rw_in[:, :], ident[0:E, 0:E])
                    nc.tensor.transpose(MB[:, 64:64 + 4 * E], gub_in[:, :], ident[0:4 * E, 0:4 * E]).then_inc(s_pw, 1)
                if n >= 3:
                    pe.wait_ge(s_te, n - 2)
                    if n - 3 < 8:
                        pe.wait_ge(s_tl, n - 2)
                for i in range(4):
                    m = 4 * n + i
                    src = gu_in[:, m, :] if m < 4 * E else dn_in[:, (m - 32) // IT, ((m - 32) % IT) * 128:((m - 32) % IT + 1) * 128]
                    last = nc.tensor.transpose(RING[n % 3][:, i * 128:(i + 1) * 128], src, ident)
                last.then_inc(s_tp, 1)

            def qkv(b, ph, k):
                f = 2 * b + (ph == "l")
                x = xn if ph == "g" else x1
                if k == 2:
                    if ph == "g":
                        pe.wait_ge(s_xn, b + 1)
                        if b > 0:
                            pe.wait_ge(s_lex, b * LJ)
                    else:
                        pe.wait_ge(s_x1, b * NP + T)
                    for h in range(2):
                        for i in range(4):
                            last = nc.tensor.transpose(bank(h)[:, i * 128:(i + 1) * 128], x[:, 4 * h + i, :], ident)
                        last.then_inc(s_xtp, 1)
                if k == 3:
                    pe.wait_ge(s_xts, 2 * f + 2)
                    if ph == "g":
                        pe.wait_ge(s_pe_, 3)
                        if b > 0:
                            pe.wait_ge(s_x1, b * NP)
                    for h in range(4):
                        for i in range(2):
                            last = nc.tensor.matmul(PRJ[h][:, i * PROJ:(i + 1) * PROJ], xT[:, (2 * h + i) * 128:(2 * h + i + 1) * 128],
                                                    wproj[ph][:, :], start=True, stop=True)
                        last.then_inc(s_prj, 1)
                if k == 8:
                    pe.wait_ge(s_stk, f + 1)
                    for t in range(T):
                        hh = t * HEADS + H
                        last = nc.tensor.transpose(KT.bitcast(fp16)[:, t * 128:(t + 1) * 128],
                                                   stk[:, hh:hh + KVH, :, :].rearrange("p a b d -> p (a b d)"), k16[:, :])
                    last.then_inc(s_kt, 1)
                if k == 8 or k == 9:
                    for h in ((0, 1) if k == 8 else (2, 3)):
                        if h == 3:
                            pe.wait_ge(s_kTs, f + 1)
                        for i in range(2):
                            for j in range(J):
                                at = i * 512 + j * 128
                                hh = (2 * h + i) * HEADS + j * KVH
                                last = nc.tensor.transpose(QT[h].bitcast(fp16)[:, at:at + 128],
                                                           stk[:, hh:hh + KVH, :, :].rearrange("p a b d -> p (a b d)"), k16[:, :])
                        last.then_inc(s_qt, 1)

            def router(b, k):
                if k == 0:
                    pe.wait_ge(s_qTs, 8 * b + 4)
                    pe.wait_ge(s_pe_, 4)
                    for t in range(T):
                        last = nc.tensor.matmul(bank(0)[:, t * E:(t + 1) * E], xT[:, t * 128:(t + 1) * 128], rwT[:, :],
                                                start=True, stop=True)
                    last.then_inc(s_lg, 1)
                if k == NR - 1:
                    pe.wait_ge(s_cw, b + 1)
                    for t in range(T):
                        last = nc.tensor.transpose(bank(0, 2)[0:E, t * 128:(t + 1) * 128], cw[:, t, :], ident)
                    last.then_inc(s_wtp, 1)

            def scores(b, u, part):
                t, kt = G_UNITS[u]
                n = b * NG + u
                if u == 0 and part == 0:
                    pe.wait_ge(s_qTs, 8 * b + 4)
                    pe.wait_ge(s_kTs, 2 * b + 1)
                    pe.wait_ge(s_wts, b + 1)
                elif u == 0:
                    if b > 0:
                        pe.wait_ge(s_gs, b * HU)
                        pe.wait_ge(s_us, b * HU)
                    else:
                        pe.wait_ge(s_te, 12)
                        pe.wait_ge(s_tl, 8)
                if u > 0:
                    pe.wait_ge(s_ex, 2 * n + part - 1)
                for c in (2 * part, 2 * part + 1):
                    last = nc.tensor.matmul(PAIR[part][:, (c % 2) * 512:(c % 2 + 1) * 512], kz[:, c, kt * 128:(kt + 1) * 128],
                                            qT[:, t, :], start=True, stop=True)
                last.then_inc(s_sc, 1)

            def pv(b, u):
                t, kt = G_UNITS[u]
                first = kt == t
                if first and t >= 2:
                    pe.wait_ge(s_o, b * NP + t - 1)
                pe.wait_ge(s_ex, 2 * (b * NG + u) + 2)
                if first:
                    pe.wait_ge(s_mk, 2 * (b * T + t) + 2)
                for c in range(KVH):
                    last = nc.tensor.matmul(OB[t % 2][32 * c:32 * c + 32, :], v[:, kt, c, :], P[:, u % 3, c * 512:(c + 1) * 512],
                                            start=first, stop=u in ENDS)
                last.then_inc(s_pv, 1)

            def o_transpose(b, p, m):
                pe.wait_ge(s_o, b * NP + p + 1)
                for j in range(J):
                    last = nc.tensor.transpose(m[:, j * 128:(j + 1) * 128], oT[:, p % 2, j * 128:(j + 1) * 128], ident)
                last.then_inc(s_ot, 1)

            def on_transpose(b, p, m):
                pe.wait_ge(s_on, b * NP + p + 1)
                nc.tensor.transpose(m[:, 0:128], on[:, p % 2, :], ident).then_inc(s_ont, 1)

            def project_out(b, p, m, ph):
                pe.wait_ge(s_ons, b * NP + p + 1)
                nc.tensor.matmul(m[:, 128:256], onT[:, p % 2, :], wo[ph][:, :], start=True, stop=True).then_inc(s_wo, 1)

            def global_step(b, u):
                if u - 2 in ENDS:
                    p = ENDS[u - 2]
                    if p >= 1:
                        pe.wait_ge(s_on, b * NP + p)
                    elif b > 0:
                        pe.wait_ge(s_yd, b * NCH)
                    o_transpose(b, p, MA)
                if u - 3 in ENDS:
                    p = ENDS[u - 3]
                    if p >= 1:
                        pe.wait_ge(s_x1, b * NP + p)
                    on_transpose(b, p, MB)
                if u + 1 < NG:
                    scores(b, u + 1, 0)
                if u - 4 in ENDS:
                    project_out(b, ENDS[u - 4], MB, "g")
                if 0 <= u - 1 < NG:
                    pv(b, u - 1)
                if u + 1 < NG:
                    scores(b, u + 1, 1)

            def local_scores(b, t, k):
                n = b * LJ + local_job(t, k)
                s = LS[k % 2]
                if k >= 2:
                    before = local_job(t, k - 2)
                elif t == 0:
                    before = None
                elif k == 1:
                    before = local_job(t - 1, 3)
                else:
                    before = local_job(t - 1, 4) if t > 1 else local_job(0, 2)
                if before is None:
                    pe.wait_ge(s_qTs, 8 * b + 8)
                    pe.wait_ge(s_kTs, 2 * b + 2)
                else:
                    pe.wait_ge(s_lex, b * LJ + before + 1)
                if k < 4:
                    last = nc.tensor.matmul(s, kz[:, k, t * 128:(t + 1) * 128], qT[:, t, :], start=True, stop=True)
                else:
                    q = qT[:, t, :].rearrange("p (j q) -> p j q", q=128)[:, :, 0:WIN]
                    for c in range(KVH):
                        last = nc.tensor.matmul(s[128 - WIN:128, c * 128:(c + 1) * 128], kz[:, c, t * 128 - WIN:t * 128], q,
                                                start=True, stop=True)
                last.then_inc(s_lsc, 1)

            def local_pv(b, t):
                if t >= 1:
                    pe.wait_ge(s_o, b * NP + T + t)
                pe.wait_ge(s_lmk, b * LJ + local_job(t, 4 if t else 3) + 1)
                for c in range(KVH):
                    last = nc.tensor.matmul(LO[32 * c:32 * c + 32, :], v[:, t, c, :], P[:, t % 3, c * 512:(c + 1) * 512],
                                            start=True, stop=t == 0)
                if t > 0:
                    for c in range(KVH):
                        last = nc.tensor.matmul(LO[32 * c:32 * c + 32, :].rearrange("p (j q) -> p j q", q=128)[:, :, 0:WIN],
                                                v[:, t - 1, c, :], Pp[:, t % 2, c * 128:(c + 1) * 128], start=False, stop=True)
                last.then_inc(s_lpv, 1)

            def local_step(b, t, k):
                if k == 0:
                    if t < T:
                        local_scores(b, t, 0)
                        local_scores(b, t, 1)
                    if t >= 2:
                        project_out(b, T + t - 2, LM, "l")
                    if 1 <= t <= T:
                        local_pv(b, t - 1)
                if k == 1:
                    if t < T:
                        local_scores(b, t, 2)
                        local_scores(b, t, 3)
                    if 1 <= t <= T:
                        pe.wait_ge(s_x1, b * NP + T + t - 1)
                        o_transpose(b, T + t - 1, LM)
                if k == 2:
                    if 1 <= t < T:
                        local_scores(b, t, 4)
                    if 1 <= t <= T:
                        on_transpose(b, T + t - 1, LM)

            def ring_free(b, i):
                if i >= 3:
                    m = (i - 3) // 2
                    pe.wait_ge(s_gs if (i - 3) % 2 == 0 else s_us, b * HU + m + 1)

            def ffn(b, n):
                def hidden(m, quarter, i, done):
                    x0 = (n // (E * IT)) * CH
                    r = RING[i % 3]
                    ring_free(b, i)
                    for k, (w, x) in enumerate(((guh, xh), (guh, xl), (gul, xh))):
                        last = nc.tensor.matmul(r, w[:, 4 * m + quarter, :], x[:, x0:x0 + CH], start=k == 0, stop=k == 2)
                    last.then_inc(done, 1)

                if n == 0:
                    pe.wait_ge(s_x1, b * NP + T)
                    pe.wait_ge(s_xl, b + 1)
                    pe.wait_ge(s_xh, b + 1)
                if n < HU:
                    e, i = (n // IT) % E, n % IT
                    hidden(e, i, 2 * n, s_g)
                    hidden(e, IT + i, 2 * n + 1, s_u)
                if n >= 2:
                    m = n - 2
                    c, r = divmod(m, E * IT)
                    if r == 0 and c > 0:
                        pe.wait_ge(s_yd, b * NCH + c)
                    pe.wait_ge(s_aw, b * HU + m + 1)
                    nc.tensor.matmul(Y, dnT[:, r, :], aw[:, m % 2, :], start=r == 0, stop=False).then_inc(s_dn, 1)
                    if r == E * IT - 1:
                        nc.tensor.matmul(Y, dnb[:, :], wT[:, c * CH:(c + 1) * CH], start=False, stop=True).then_inc(s_y, 1)

            def y_back(b, c):
                pe.wait_ge(s_ys, b * NCH + c + 1)
                for i in range(4):
                    last = nc.tensor.transpose(Y[:, i * 128:(i + 1) * 128], yT[:, i * 128:(i + 1) * 128], ident)
                last.then_inc(s_yt, 1)

            steps = {"Q": qkv, "R": router, "G": global_step, "L": local_step, "F": ffn, "Y": y_back, "W": weights, "O": None}
            for kind, *args in SCHEDULE:
                if steps[kind]:
                    steps[kind](*args)

        @block.scalar
        def _(act):
            def weights(b, n):
                act.wait_ge(s_tp, n + 1)
                if n < 8:
                    nc.scalar.activation(guh[:, 4 * n:4 * n + 4, :].rearrange("p a b -> p (a b)"), RING[n % 3], ACT.Copy,
                                         scale=WSCALE).then_inc(s_te, 1)
                else:
                    m = 4 * (n - 8)
                    nc.scalar.activation(dnT[:, m:m + 4, :].rearrange("p a b -> p (a b)"), RING[n % 3], ACT.Copy,
                                         scale=0.5 / ACC).then_inc(s_te, 1)

            def qkv(b, ph, k):
                f = 2 * b + (ph == "l")
                if k == 2:
                    for h in range(2):
                        act.wait_ge(s_xtp, 2 * f + h + 1)
                        if h == 0 and f > 0:
                            act.wait_ge(s_prj, 4 * f)
                            act.wait_ge(s_lg, (f + 1) // 2)
                            act.wait_ge(s_xl, (f + 1) // 2)
                        nc.scalar.activation(xT[:, h * 512:(h + 1) * 512], bank(h), ACT.Copy).then_inc(s_xts, 1)
                if k == 5:
                    act.wait_ge(s_rot, f + 1)
                    nc.scalar.activation(rtmp[:, :, :], rot[:, :, :], ACT.Square).then_inc(s_sq, 1)
                if k == 8 or k == 9:
                    for h in ((0, 1) if k == 8 else (2, 3)):
                        act.wait_ge(s_qt, 4 * f + h + 1)
                        nc.scalar.activation(qT[:, 2 * h:2 * h + 2, :].rearrange("p a b -> p (a b)"), QT[h].bitcast(fp16),
                                             ACT.Copy).then_inc(s_qTs, 1)

            def router(b, k):
                if k == 1:
                    act.wait_ge(s_lx, b + 1)
                    nc.scalar.activation(cw[:, :, :], lg[:, :, :], ACT.Exp).then_inc(s_le, 1)
                if k == NR - 1:
                    if b > 0:
                        act.wait_ge(s_u, b * HU)
                    act.wait_ge(s_xts, 4 * b + 2)
                    nc.scalar.activation(xh[:, :], xT[:, :], ACT.Copy, scale=WSCALE).then_inc(s_xh, 1)

            def global_step(b, u):
                if 0 <= u < NG:
                    n = b * NG + u
                    for part in range(2):
                        act.wait_ge(s_sc, 2 * n + part + 1)
                        if part == 0 and u >= 3:
                            act.wait_ge(s_pv, n - 2)
                        nc.scalar.activation(P[:, u % 3, part * 1024:(part + 1) * 1024], PAIR[part], ACT.Exp,
                                             scale=EXP_SCALE).then_inc(s_ex, 1)

            def local_step(b, t, k):
                if t >= T or (k == 2 and t == 0):
                    return
                if k == 0 and t == 0:
                    act.wait_ge(s_pv, (b + 1) * NG)
                if k == 0 and t >= 3:
                    act.wait_ge(s_lpv, b * T + t - 2)
                for j in ((0, 1), (2, 3), (4,))[k]:
                    act.wait_ge(s_lsc, b * LJ + local_job(t, j) + 1)
                    if j < 4:
                        nc.scalar.activation(P[:, t % 3, j * 512:(j + 1) * 512], LS[j % 2], ACT.Exp, scale=EXP_SCALE).then_inc(s_lex, 1)
                    else:
                        nc.scalar.activation(Pp[128 - WIN:128, t % 2, :], LS[0][128 - WIN:128, :], ACT.Exp,
                                             scale=EXP_SCALE).then_inc(s_lex, 1)

            def ffn(b, n):
                if n < HU:
                    e, i = (n // IT) % E, n % IT
                    g = b * HU + n
                    act.wait_ge(s_u, g + 1)
                    if n >= 2:
                        act.wait_ge(s_aw, g - 1)
                    nc.scalar.activation(up[:, n % 2, :], RING[(2 * n + 1) % 3], ACT.Identity, scale=1.0 / ACC,
                                         bias=gub[:, e, IT + i:IT + i + 1]).then_inc(s_us, 1)
                    act.wait_ge(s_gs, g + 1)
                    if n >= 2:
                        act.wait_ge(s_a, g - 1)
                    nc.scalar.activation(sig[:, n % 2, :], gate[:, n % 2, :], ACT.Tanh, scale=ALPHA / 2 / ACC).then_inc(s_th, 1)

            def y_back(b, c):
                g = b * NCH + c
                act.wait_ge(s_y, g + 1)
                nc.scalar.activation(yT[:, :], Y, ACT.Copy).then_inc(s_ys, 1)
                act.wait_ge(s_yt, g + 1)
                if c == 0 and b > 0:
                    act.wait_ge(s_st, b * NCH * 16)
                nc.scalar.activation(ys[:, c * CH // 128:(c + 1) * CH // 128, :].rearrange("p t d -> p (t d)"), Y, ACT.Tanh,
                                     scale=0.5).then_inc(s_yth, 1)

            steps = {"Q": qkv, "R": router, "G": global_step, "L": local_step, "F": ffn, "Y": y_back, "W": weights, "O": None}
            for kind, *args in SCHEDULE:
                if steps[kind]:
                    steps[kind](*args)

        @block.gpsimd
        def _(pool):
            nc.gpsimd.memset(kz[:, :, :], 0.0).then_inc(s_zero, 1)
            nc.gpsimd.memset(v[:, :, :, :], 0.0).then_inc(s_plink, 1)
            nc.gpsimd.memset(Pp[:, :, :], 0.0).then_inc(s_zero, 1)
            pool.wait_ge(s_plink, 1)
            nc.gpsimd.memset(v[:, :, :, HD:HD + 1], 1.0).then_inc(s_zero, 1)

            def qkv(b, ph, k):
                f = 2 * b + (ph == "l")
                if k == 3:
                    pool.wait_ge(s_pev, 4 * f + 4)
                    if f > 0:
                        pool.wait_ge(s_stk, f)
                    heads = lambda a: a[:, :, :].rearrange("p (t h) d -> p t h d", t=T)
                    cos = rope[ph][:, 0:T * HD].rearrange("p (t o d) -> p t o d", t=T, o=1).to_broadcast([128, T, HEADS, HD])
                    nc.gpsimd.tensor_tensor(heads(rot), heads(qk), cos, ALU.mult).then_inc(s_cos, 1)

            def global_step(b, u):
                if 0 <= u < NG and G_UNITS[u][0] == G_UNITS[u][1]:
                    for part in range(2):
                        pool.wait_ge(s_ex, 2 * (b * NG + u) + part + 1)
                        p = P[:, u % 3, part * 1024:(part + 1) * 1024].rearrange("p (h q) -> p h q", q=128)
                        nc.gpsimd.affine_select(out=p, in_=p, compare_op=ALU.is_ge, fill=0.0, base=0,
                                                pattern=[[0, 8], [1, 128]], channel_multiplier=-1).then_inc(s_mk, 1)

            def local_step(b, t, k):
                if t >= T or (k == 2 and t == 0):
                    return
                for j in ((0, 1), (2, 3), (4,))[k]:
                    n = b * LJ + local_job(t, j)
                    pool.wait_ge(s_lex, n + 1)
                    if j < 4:
                        p = P[:, t % 3, j * 512:(j + 1) * 512].rearrange("p (h q) -> p h q", q=128)
                        nc.gpsimd.affine_select(out=p, in_=p, compare_op=ALU.is_ge, fill=0.0, base=0,
                                                pattern=[[0, J], [1, 128]], channel_multiplier=-1).then_inc(s_plink, 1)
                        pool.wait_ge(s_plink, 2 + 4 * (b * T + t) + j)
                        nc.gpsimd.affine_select(out=p, in_=p, compare_op=ALU.is_ge, fill=0.0, base=WIN - 1,
                                                pattern=[[0, J], [-1, 128]], channel_multiplier=1).then_inc(s_lmk, 1)
                    else:
                        p = Pp[:, t % 2, :].rearrange("p (h q) -> p h q", q=WIN)
                        nc.gpsimd.affine_select(out=p, in_=p, compare_op=ALU.is_ge, fill=0.0, base=WIN - 129,
                                                pattern=[[0, H], [-1, WIN]], channel_multiplier=1).then_inc(s_lmk, 1)

            def ffn(b, n):
                if n == 0:
                    pool.wait_ge(s_wb, 16 * (b + 1))
                if 1 <= n <= HU:
                    m = n - 1
                    e, c = (m // IT) % E, m // (E * IT)
                    pool.wait_ge(s_a, b * HU + m + 1)
                    if m >= 2:
                        pool.wait_ge(s_dn, b * HU + m - 1)
                    nc.gpsimd.tensor_tensor(aw[:, m % 2, :], up[:, m % 2, :], wb[:, e * S + c * CH:e * S + (c + 1) * CH],
                                            ALU.mult).then_inc(s_aw, 1)

            steps = {"Q": qkv, "R": None, "G": global_step, "L": local_step, "F": ffn, "Y": None, "W": None, "O": None}
            for kind, *args in SCHEDULE:
                if steps[kind]:
                    steps[kind](*args)

        @block.vector
        def _(dve):
            linked = [0]

            def link(ins):
                ins.then_inc(s_link, 1)
                linked[0] += 1
                dve.wait_ge(s_link, linked[0])

            def rsqrt(y, x, n):
                t0, t1 = ntmp[:, 0, 0:n], ntmp[:, 1, 0:n]
                link(nc.vector.tensor_scalar(y.bitcast(i32), x.bitcast(i32), -0.5, MAGIC, ALU.mult, ALU.add))
                for _ in range(3):
                    link(nc.vector.scalar_tensor_tensor(t0, y, -0.5, y, ALU.mult, ALU.mult))
                    link(nc.vector.tensor_tensor(t1, t0, x, ALU.mult))
                    link(nc.vector.scalar_tensor_tensor(y, t1, 1.5, y, ALU.add, ALU.mult))

            def bcast(ap, n):
                m = ap.shape[1]
                return ap.rearrange("p (m o) -> p m o", o=1).to_broadcast([128, m, n])

            def weights(b, n):
                if n == 0:
                    for ph in ("g", "l"):
                        last = nc.vector.tensor_scalar(wproj[ph][:, 0:H * HD].rearrange("p (j c d) -> p j c d", j=J, c=KVH),
                                                       wq_in[ph][:, :].rearrange("p (c j d) -> p j c d", j=J, c=KVH),
                                                       norm_w[ph][:, 0:1], None, ALU.mult)
                    nc.vector.tensor_scalar(wproj["l"][:, H * HD:PROJ], wkv_in[:, :], norm_w["l"][:, 0:1], None, ALU.mult) \
                        .then_inc(s_pe_, 1)
                if n == 1:
                    dve.wait_ge(s_pw, 3)
                    nc.vector.tensor_copy(rwT[:, :], MB[:, 0:E]).then_inc(s_pe_, 1)
                    bT = MB[:, 64:64 + 4 * E].rearrange("p (e m) -> p e m", m=4)
                    nc.vector.tensor_scalar(gub[:, :, 0:IT], bT[:, :, 0:IT], ACC, None, ALU.mult).then_inc(s_pe_, 1)
                    nc.vector.tensor_scalar(gub[:, :, IT:2 * IT], bT[:, :, IT:2 * IT], 1.0, None, ALU.add).then_inc(s_pe_, 1)
                if 1 <= n <= 8:
                    m = n - 1
                    dve.wait_ge(s_te, m + 1)
                    nc.vector.scalar_tensor_tensor(gul[:, 4 * m:4 * m + 4, :].rearrange("p a b -> p (a b)"), RING[m % 3], WSCALE,
                                                   guh[:, 4 * m:4 * m + 4, :].rearrange("p a b -> p (a b)"), ALU.mult,
                                                   ALU.subtract).then_inc(s_tl, 1)

            def layernorm(b, k):
                if k == 0:
                    dve.wait_ge(s_x[b], 16)
                    for t in range(T):
                        last = nc.vector.bn_stats(stats[:, t, :], xs[:, b, t, :])
                    link(last)
                    for t in range(T):
                        last = nc.vector.bn_aggr(mv[:, t, :], stats[:, t, :])
                    link(last)
                    link(nc.vector.tensor_scalar(rs[:, 2, :], mv[:, :, 1], LN_EPS, None, ALU.add))
                if k == 1:
                    rsqrt(rs[:, 0, :], rs[:, 2, :], T)
                    if b > 0:
                        dve.wait_ge(s_xtp, 4 * b - 2)
                    for t in range(T):
                        last = nc.vector.tensor_scalar(xn[:, t, :], xs[:, b, t, :], mv[:, t, 0:1], rs[:, 0, t:t + 1],
                                                       ALU.subtract, ALU.mult)
                    last.then_inc(s_xn, 1)
                if k == 2:
                    link(nc.vector.tensor_tensor(rs[:, 3, :], rs[:, 0, :], rs[:, 0, :], ALU.mult))
                    link(nc.vector.tensor_tensor(rs[:, 3, :], rs[:, 3, :], mv[:, :, 1], ALU.mult))
                    link(nc.vector.tensor_scalar(rs[:, 3, :], rs[:, 3, :], RMS_EPS, None, ALU.add))
                    rsqrt(rs[:, 1, :], rs[:, 3, :], T)

            def rms(b):
                sq = rtmp[:, 0:T * 16, :].rearrange("p (t a) d -> p t (a d)", t=T)
                dve.wait_ge(s_x1, b * NP + T)
                link(nc.vector.tensor_tensor(sq, x1[:, :, :], x1[:, :, :], ALU.mult))
                link(nc.vector.tensor_reduce(rs[:, 2, :], sq, AXX, ALU.add))
                link(nc.vector.tensor_scalar(rs[:, 3, :], rs[:, 2, :], 1.0 / D, RMS_EPS, ALU.mult, ALU.add))
                rsqrt(rs[:, 1, :], rs[:, 3, :], T)

            flat = lambda a: a[:, :, :].rearrange("p a d -> p (a d)")

            def qkv(b, ph, k):
                f = 2 * b + (ph == "l")
                if ph == "g":
                    layernorm(b, k)
                elif k == 2:
                    rms(b)
                if k == 3:
                    if f == 0:
                        dve.wait_ge(s_zero, 3)
                    for h in range(4):
                        dve.wait_ge(s_prj, 4 * f + h + 1)
                        src = PRJ[h][:, 0:2 * PROJ].rearrange("p (t n) -> p t n", t=2)
                        r = rs[:, 1, 2 * h:2 * h + 2]
                        nc.vector.tensor_tensor(qk[:, 2 * h * HEADS:(2 * h + 2) * HEADS, :].rearrange("p (t a) d -> p t (a d)", t=2),
                                                src[:, :, 0:QK], bcast(r, QK), ALU.mult)
                        nc.vector.tensor_tensor(v[:, 2 * h:2 * h + 2, :, 0:HD], src[:, :, QK:PROJ].rearrange("p t (c d) -> p t c d", c=KVH),
                                                r.rearrange("p (t o q) -> p t o q", o=1, q=1).to_broadcast([128, 2, KVH, HD]), ALU.mult) \
                            .then_inc(s_pev, 1)
                if k == 4:
                    dve.wait_ge(s_pev, 4 * f + 4)
                    sin = rope[ph][:, T * HD:2 * T * HD].rearrange("p (t o d w) -> p t o d w", t=T, o=1, w=2)
                    q5 = qk[:, :, :].rearrange("p (t h) (d w) -> p t h d w", t=T, w=2)
                    r5 = rtmp[:, :, :].rearrange("p (t h) (d w) -> p t h d w", t=T, w=2)
                    nc.vector.tensor_tensor(r5[:, :, :, :, 0], q5[:, :, :, :, 1], sin[:, :, :, :, 0].to_broadcast([128, T, HEADS, HD // 2]), ALU.mult)
                    link(nc.vector.tensor_tensor(r5[:, :, :, :, 1], q5[:, :, :, :, 0], sin[:, :, :, :, 1].to_broadcast([128, T, HEADS, HD // 2]), ALU.mult))
                if k == 5:
                    dve.wait_ge(s_cos, f + 1)
                    nc.vector.tensor_tensor(flat(rot), flat(rot), flat(rtmp), ALU.add).then_inc(s_rot, 1)
                if k == 6:
                    dve.wait_ge(s_sq, f + 1)
                    link(nc.vector.tensor_reduce(msq[:, :], rtmp[:, :, :], AXX, ALU.add))
                    c = 1.0 / (QKSCALE * QKSCALE)
                    link(nc.vector.tensor_scalar(msq[:, :], msq[:, :], c / HD, c * RMS_EPS, ALU.mult, ALU.add))
                    rsqrt(rn[:, :], msq[:, :], T * HEADS)
                if k == 7:
                    link(nc.vector.tensor_tensor(rot[:, :, :], rot[:, :, :], bcast(rn[:, :], HD), ALU.mult))
                    link(nc.vector.tensor_copy(stk[:, :, 0, :], rot[:, :, :]))
                if k == 8:
                    link(nc.vector.tensor_tensor(stk[:, :, 3, :], rot[:, :, :], stk[:, :, 0, :], ALU.subtract))
                    st = stk[:, :, :, :].rearrange("p (t h) w d -> p t h w d", t=T)
                    nc.vector.tensor_copy(st[:, :, 0:H, 1, :], st[:, :, 0:H, 0, :])
                    nc.vector.tensor_copy(st[:, :, 0:H, 2, :], st[:, :, 0:H, 3, :])
                    nc.vector.tensor_copy(st[:, :, H:HEADS, 1, :], st[:, :, H:HEADS, 3, :])
                    nc.vector.tensor_copy(st[:, :, H:HEADS, 2, :], st[:, :, H:HEADS, 0, :]).then_inc(s_stk, 1)
                if k == 9:
                    dve.wait_ge(s_kt, f + 1)
                    for c in range(KVH):
                        last = nc.vector.tensor_copy(kz[32 * c:32 * c + 32, c, :], KT.bitcast(fp16)[32 * c:32 * c + 32, :])
                    last.then_inc(s_kTs, 1)

            def router(b, k):
                lgf = lg[:, :, :].rearrange("p t e -> p (t e)")
                n = T * E * E
                gt, eq = pair_gt, pair_eq
                if k == 0:
                    dve.wait_ge(s_lg, b + 1)
                    rbb = rb[:, :].rearrange("p (o e) -> p o e", o=1).to_broadcast([128, T, E])
                    link(nc.vector.tensor_tensor(lg[:, :, :], bank(0)[:, 0:T * E].rearrange("p (t e) -> p t e", e=E), rbb, ALU.add))
                    mine = bcast(lgf, E).rearrange("p (t e) f -> p t e f", t=T)
                    other = lg[:, :, :].rearrange("p t (o e) -> p t o e", o=1).to_broadcast([128, T, E, E])
                    cube = lambda a: a.rearrange("p (t e f) -> p t e f", t=T, e=E)
                    nc.vector.tensor_tensor(cube(gt), other, mine, ALU.is_gt)
                    link(nc.vector.tensor_tensor(cube(eq), other, mine, ALU.is_equal))
                    link(nc.vector.tensor_reduce(mx[:, 0, :], lg[:, :, :], AXX, ALU.max))
                    nc.vector.tensor_tensor(lg[:, :, :], lg[:, :, :], bcast(mx[:, 0, :], E), ALU.subtract).then_inc(s_lx, 1)
                if k == 1:
                    before = earlier.rearrange("p (o e) -> p o e", o=1).to_broadcast([128, T, E * E])
                    rows = eq.rearrange("p (t e) -> p t e", t=T)
                    link(nc.vector.tensor_tensor(rows, rows, before, ALU.mult))
                    link(nc.vector.tensor_tensor(gt, gt, eq, ALU.add))
                    link(nc.vector.tensor_reduce(rank[:, :], gt.rearrange("p (a f) -> p a f", f=E), AXX, ALU.add))
                if k == 2:
                    dve.wait_ge(s_le, b + 1)
                    cwf = cw[:, :, :].rearrange("p t e -> p (t e)")
                    link(nc.vector.scalar_tensor_tensor(cwf, rank[:, :], TOPK - 0.5, cwf, ALU.is_lt, ALU.mult))
                    link(nc.vector.tensor_reduce(mx[:, 0, :], cw[:, :, :], AXX, ALU.add))
                    link(nc.vector.reciprocal(mx[:, 1, :], mx[:, 0, :]))
                    nc.vector.tensor_tensor(cw[:, :, :], cw[:, :, :], bcast(mx[:, 1, :], E), ALU.mult).then_inc(s_cw, 1)
                if k == NR - 1:
                    dve.wait_ge(s_wtp, b + 1)
                    if b > 0:
                        dve.wait_ge(s_y, b * NCH)
                        dve.wait_ge(s_wst, b * 16)
                    nc.vector.tensor_copy(wT[:, :], bank(0, 2)[0:E, :]).then_inc(s_wts, 1)
                    dve.wait_ge(s_xh, b + 1)
                    nc.vector.scalar_tensor_tensor(xl[:, :], xT[:, :], WSCALE, xh[:, :], ALU.mult, ALU.subtract).then_inc(s_xl, 1)

            def o_evacuate(b, p, src):
                nc.vector.tensor_copy(oT[:, p % 2, :], src).then_inc(s_o, 1)

            def o_normalise(b, p, m):
                dve.wait_ge(s_ot, b * NP + p + 1)
                o = m.rearrange("p (j c d) -> p j c d", j=J, c=KVH)
                link(nc.vector.reciprocal(rec[:, p % 2, :].rearrange("p (j c) -> p j c", j=J), o[:, :, :, HD]))
                nc.vector.tensor_tensor(on[:, p % 2, :].rearrange("p (c j d) -> p j c d", c=KVH, j=J), o[:, :, :, 0:HD],
                                        rec[:, p % 2, :].rearrange("p (j c o) -> p j c o", j=J, o=1).to_broadcast([128, J, KVH, HD]),
                                        ALU.mult).then_inc(s_on, 1)

            def on_evacuate(b, p, m):
                dve.wait_ge(s_ont, b * NP + p + 1)
                nc.vector.tensor_copy(onT[:, p % 2, :], m[:, 0:128]).then_inc(s_ons, 1)

            def residual(b, p, m):
                dve.wait_ge(s_wo, b * NP + p + 1)
                src, dst = (xn, x1) if p < T else (x1, ss)
                nc.vector.tensor_tensor(dst[:, p % T, :], m[:, 128:256], src[:, p % T, :], ALU.add).then_inc(s_x1, 1)

            def global_step(b, u):
                if u - 2 in ENDS:
                    o_normalise(b, ENDS[u - 2], MA)
                if u - 3 in ENDS:
                    on_evacuate(b, ENDS[u - 3], MB)
                if u - 4 in ENDS:
                    residual(b, ENDS[u - 4], MB)
                if u - 1 in ENDS:
                    p = ENDS[u - 1]
                    dve.wait_ge(s_pv, b * NG + u)
                    o_evacuate(b, p, OB[p % 2])

            def local_step(b, t, k):
                if k == 0:
                    if t >= 2:
                        residual(b, T + t - 2, LM)
                    if 1 <= t <= T:
                        dve.wait_ge(s_lpv, b * T + t)
                        o_evacuate(b, T + t - 1, LO)
                if k == 1 and 1 <= t <= T:
                    o_normalise(b, T + t - 1, LM)
                if k == 2 and 1 <= t <= T:
                    on_evacuate(b, T + t - 1, LM)

            def ffn(b, n):
                if n < HU:
                    e, i = (n // IT) % E, n % IT
                    dve.wait_ge(s_g, b * HU + n + 1)
                    nc.vector.tensor_scalar(gate[:, n % 2, :], RING[(2 * n) % 3], gub[:, e, i:i + 1], ACC * LIMIT, ALU.add,
                                            ALU.min).then_inc(s_gs, 1)
                if 1 <= n <= HU:
                    m = n - 1
                    dve.wait_ge(s_us, b * HU + m + 1)
                    nc.vector.tensor_scalar(up[:, m % 2, :], up[:, m % 2, :], 1.0 + LIMIT, 1.0 - LIMIT, ALU.min, ALU.max)
                    dve.wait_ge(s_th, b * HU + m + 1)
                    link(nc.vector.scalar_tensor_tensor(sig[:, m % 2, :], sig[:, m % 2, :], 1.0, gate[:, m % 2, :], ALU.add, ALU.mult))
                    nc.vector.tensor_tensor(up[:, m % 2, :], up[:, m % 2, :], sig[:, m % 2, :], ALU.mult).then_inc(s_a, 1)

            def y_back(b, c):
                g = b * NCH + c
                dve.wait_ge(s_yth, g + 1)
                y = ys[:, c * CH // 128:(c + 1) * CH // 128, :].rearrange("p t d -> p (t d)")
                nc.vector.scalar_tensor_tensor(y, y, 1.0, Y, ALU.add, ALU.mult).then_inc(s_yd, 1)

            def result(b, c):
                ts = slice(c * CH // 128, (c + 1) * CH // 128)
                part = lambda a: a.rearrange("p t d -> p (t d)")
                y = part(ys[:, ts, :])
                dve.wait_ge(s_x1, b * NP + NP)
                dve.wait_ge(s_yd, b * NCH + c + 1)
                link(nc.vector.scalar_tensor_tensor(y, y, 0.5, part(ss[:, ts, :]), ALU.mult, ALU.mult))
                nc.vector.tensor_tensor(y, y, part(xs[:, b, ts, :]), ALU.add).then_inc(s_out, 1)

            pair_gt, pair_eq = flat(rtmp)[:, 0:T * E * E], flat(rtmp)[:, T * E * E:2 * T * E * E]
            dve.wait_ge(s_pw, 1)
            nc.vector.tensor_copy(kvdT[:, :], MB[0:32, 0:128]).then_inc(s_pe_, 1)
            dve.wait_ge(s_pw, 2)
            nc.vector.tensor_scalar(wproj["g"][:, H * HD:PROJ], MB[:, 128:192], norm_w["g"][:, 0:1], None, ALU.mult).then_inc(s_pe_, 1)

            steps = {"Q": qkv, "R": router, "G": global_step, "L": local_step, "F": ffn, "Y": y_back, "W": weights, "O": result}
            for kind, *args in SCHEDULE:
                if steps[kind]:
                    steps[kind](*args)


_INS = ["L0_attn_hidden", "L0_attn_norm1_w", "L0_attn_norm2_w", "L0_attn_g_wq", "L0_attn_g_kv_down", "L0_attn_g_k_up",
        "L0_attn_g_v_up", "L0_attn_g_wo", "L0_attn_l_wq", "L0_attn_l_wk", "L0_attn_l_wv", "L0_attn_l_wo",
        "L0_ffn_router_weight", "L0_ffn_router_bias", "L0_ffn_gate_up_proj", "L0_ffn_gate_up_proj_bias",
        "L0_ffn_down_proj", "L0_ffn_down_proj_bias"]


def _constants():
    import numpy as np
    f = np.float32
    parts = [np.eye(128, dtype=f), np.tile(np.tril(np.ones((E, E), f), -1).reshape(1, -1), (128, 1))]
    for base in (1000000.0, 10000.0):
        inv = (f(1.0) / f(base) ** (np.arange(0, HD, 2, dtype=f) / f(HD))).astype(f)
        ang = np.arange(S, dtype=f)[:, None] * inv[None, :]
        cos, sin = np.cos(ang), np.sin(ang)
        for a in (np.stack([cos, cos], -1), np.stack([-sin, sin], -1)):
            parts.append(a.reshape(T, 128, HD).transpose(1, 0, 2).reshape(128, T * HD).astype(f))
    return np.ascontiguousarray(np.concatenate(parts, 1)), np.eye(128, dtype=np.float16)


def kernel(**inputs):
    import numpy as _np
    import concourse.bacc as _bacc
    from concourse import mybir as _mybir
    from concourse.bass_utils import run_bass_kernel_spmd as _run

    nc = _bacc.Bacc("TRN2", target_bir_lowering=False, num_devices=1)
    arrays, args = {}, []
    c32, c16 = _constants()
    for name, a in [(n, _np.ascontiguousarray(inputs[n])) for n in _INS] + [("const32", c32), ("const16", c16)]:
        arrays[f"in_{name}_dram"] = a
        args.append(nc.dram_tensor(f"in_{name}_dram", a.shape, _mybir.dt.from_np(a.dtype), kind="ExternalInput").ap())
    args.append(nc.dram_tensor("out_0_dram", (B, S, D), _mybir.dt.float32, kind="ExternalOutput").ap())
    gated_attention_moe_kernel(nc, *args)
    r = _run(nc, [arrays], core_ids=[0])
    return r.results[0]["out_0_dram"]
```

```python
import concourse.bass as bass
from concourse import mybir
from contextlib import ExitStack

B, S, D = 2, 1024, 128
T = S // 128
H, KVH, HD = 16, 4, 8
J = H // KVH
WIN = 32
E, I = 8, 256
TOPK = 4
LIMIT, ALPHA = 7.0, 1.702
LN_EPS, RMS_EPS = 1e-5, 1e-6
HEADS = H + KVH
QK = HEADS * HD
PROJ = QK + KVH * HD
PARTS = 4
QKSCALE = 64.0
EXP_SCALE = 1.0 / (QKSCALE * QKSCALE * HD ** 0.5)
MAGIC = float(0x5F3759DF)
CH = 512
NCH = S // CH
IT = I // 128
WSCALE = 32.0
ACC = WSCALE * WSCALE
HU = NCH * E * IT
FIRST_FILLS = 53
DOWN_LAG = 3
UNITS = [(b, t, kt) for b in range(B) for t in range(T) for kt in [t] + list(range(t))]
NU, NG = len(UNITS), len(UNITS) // B
ENDS = {u: UNITS[u][0] * T + UNITS[u][1] for u in range(NU) if u + 1 == NU or UNITS[u + 1][:2] != UNITS[u][:2]}
LAG = 2
TURNS = {}
for end, tile in sorted(ENDS.items()):
    TURNS[max([end + 4] + [step + 2 * LAG for step in TURNS])] = tile
STAGES = [(b, ph) for ph in ("g", "l") for b in range(B)]
BETWEEN = range(1, 6)
HT = T // 2
HH = HT * HEADS
LJ = 5 * T - 1
NL = 5
Q_STEPS = ("stats", "std", "norm", "xT", "project0", "project1", "logits", "rope", "newton1", "newton2",
           "rotate", "split", "kT", "qT0", "qT1")
R_STEPS = ("compare", "max", "rank", "choose", "weigh", "wT0", "wT1")
NW = (4 * E + 2 * E) // 4
NGUW = E


def local_job(t, k):
    return 5 * t + k - (1 if t > 0 else 0)


def schedule():
    def spread(main, side):
        out, at = [], 0
        for i, m in enumerate(main):
            to = (i + 1) * len(side) // len(main)
            out += [m] + side[at:to]
            at = to
        return out

    def Q(qh, first="stats", last="qT1"):
        return [("Q", qh, k) for k in Q_STEPS[Q_STEPS.index(first):Q_STEPS.index(last) + 1]]

    def R(b, first="compare", last="wT1"):
        return [("R", b, k) for k in R_STEPS[R_STEPS.index(first):R_STEPS.index(last) + 1]]

    def G(lo, hi):
        return [("G", u) for u in range(lo, hi)]

    def result(b):
        return [("O", b * NCH + c) for c in range(NCH)]

    steps = []
    weights = [("W", n) for n in range(NW + 1)]
    lows = [("V", n) for n in range(NGUW)]
    steps += Q(0, "stats", "std") + Q(0, "norm", "xT") + [("P",)] + Q(1, "stats", "stats") + Q(0, "project0", "project1")
    steps += spread(Q(0, "rope", "rope") + Q(0, "logits", "logits") + Q(0, "newton1", "rotate"), weights[:NW])
    steps += Q(0, "split", "qT0") + Q(1, "std", "norm") + weights[NW:]
    between = [[] for _ in range(NU + 3)]

    def place(at, groups):
        for i, group in enumerate(groups):
            between[at + i] += group

    def one_by_one(items):
        return [[item] for item in items]

    place(1, [Q(0, "qT1")])
    place(1, one_by_one(Q(1, "xT", "project1")) + [Q(1, "logits", "rope"), Q(1, "newton1", "newton2"), Q(1, "rotate", "split")]
          + one_by_one(Q(1, "kT")))
    for i, low in enumerate(lows):
        place(12 + 3 * i, [[low]])
    place(9, [Q(2, "stats", "stats"), Q(2, "std", "std"), [], Q(2, "norm", "norm")])
    at = 13
    for qh in range(2, 6):
        if qh == 4:
            place(at, one_by_one(R(0, "wT0")))
            at += 2
        place(at, one_by_one(Q(qh, "xT", "project1") + (Q(qh, "logits", "logits") if qh < 4 else []) + Q(qh, "rope", "split")) + [[], []]
              + one_by_one(Q(qh, "kT")))
        length = 14 if qh < 4 else 13
        if qh < 5:
            place(at + length - 5, one_by_one(Q(qh + 1, "stats", "std")) + [[], Q(qh + 1, "norm", "norm")])
        if qh in (3, 5):
            place(at, one_by_one(R(qh // 4, "compare", "weigh")))
        at += length
    place(at, one_by_one(R(1, "wT0")))
    for u in range(-1, NU + 2):
        steps += [("G", u)] + between[u + 1]
    fills = []
    for n in range(B * HU + DOWN_LAG):
        fills += [("F", n, 0), ("F", n, 1)]
        g, r = divmod(n - DOWN_LAG, E * IT)
        if n >= DOWN_LAG and r == E * IT - 1:
            fills += [("Y", g, 0), ("Y", g, 1)]
    local = [[("L", t, k) for k in range(NL)] for t in range(B * T + 1)] + [[("L", B * T + 1, k) for k in range(2)]]
    first = G(NU + 2, max(TURNS) + 2 * LAG + 1) + spread(sum(local[:T], []), Q(6) + Q(7))
    second = local[T] + local[T + 1][:2] + result(0) + local[T + 1][2:] + sum(local[T + 2:], [])
    at = len(fills) * FIRST_FILLS // 100
    steps += spread(fills[:at], first) + spread(fills[at:], second)
    steps += result(B - 1)
    return steps


def gated_attention_moe_kernel(nc, hidden, n1, n2, g_wq, g_kvd, g_ku, g_vu, g_wo, l_wq, l_wk, l_wv, l_wo,
                               r_w, r_b, gu_w, gu_b, dn_w, dn_b, c32, c16, out):
    fp32, fp16, i32 = mybir.dt.float32, mybir.dt.float16, mybir.dt.int32
    ALU = mybir.AluOpType
    ACT = mybir.ActivationFunctionType
    AXX = mybir.AxisListType.X
    SCHEDULE = schedule()

    ctx = ExitStack()
    with ctx:
        def sb(name, shape, dt=fp32):
            return ctx.enter_context(nc.sbuf_tensor(name, shape, dt))

        def sem(name):
            return ctx.enter_context(nc.semaphore(name))

        k32 = sb("k32", [128, c32.shape[1]])
        ident = k32[:, 0:128]
        earlier = k32[:, 128:192]
        rope = {"g": k32[:, 192:320], "l": k32[:, 320:448]}
        k16 = sb("k16", [128, 128], fp16)
        wq_in = {"g": sb("wq_g", [128, H * HD]), "l": sb("wq_l", [128, H * HD])}
        wkv_in = sb("wkv_in", [128, 2 * KVH * HD])
        kvd = sb("kvd", [128, 32])
        kvdT = sb("kvdT", [32, 128])
        kvu = sb("kvu", [32, 2 * KVH * HD])
        norm_w = {"g": sb("n1w", [128, 1]), "l": sb("n2w", [128, 1])}
        wproj = {"g": sb("wproj_g", [128, PROJ]), "l": sb("wproj_l", [128, PROJ])}
        wo = {"g": sb("wo_g", [128, D]), "l": sb("wo_l", [128, D])}
        rw_in = sb("rw_in", [E, D])
        rwT = sb("rwT", [128, E])
        rb = sb("rb", [128, E])
        gub_in = sb("gub_in", [4 * E, 128])
        gub = sb("gub", [128, E, 2 * IT])
        guh = sb("guh", [128, 4 * E, 128], fp16)
        gul = sb("gul", [128, 4 * E, 128], fp16)
        dnT = sb("dnT", [128, 2 * E, D])
        dnb = sb("dnb", [E, D])

        xs = sb("xs", [128, B, T, D])
        x = sb("x", [128, B, T, D])
        xT = sb("xT", [128, HT * 128])
        xh = sb("xh", [128, B, S], fp16)
        xl = sb("xl", [128, B, S], fp16)
        xsq = sb("xsq", [128, HT, D])
        stats = sb("stats", [128, HT, 6])
        mv = sb("mv", [128, HT, 2])
        rs = sb("rs", [128, 2, 4, HT])
        ntmp = sb("ntmp", [128, 2, HH])
        qk = sb("qk", [128, HH, HD])
        rot = sb("rot", [128, HH, HD])
        rtmp = sb("rtmp", [128, HH, HD])
        sq = sb("sq", [128, HH, HD])
        msq = sb("msq", [128, HH])
        rn = sb("rn", [128, HH])
        stk = sb("stk", [128, HH, PARTS, HD], fp16)
        qT = sb("qT", [128, B, T, J * 128], fp16)
        kz = sb("kz", [128, B, KVH, S], fp16)
        v = sb("v", [128, B, T, KVH, 32])
        P = sb("P", [128, 4, KVH * 512])
        Pp = sb("Pp", [128, 2, 512])
        oT = sb("oT", [128, 3, 512])
        on = sb("on", [128, 2, 128])
        onT = sb("onT", [128, 2, 128])
        rec = sb("rec", [128, 2, H])
        lg = sb("lg", [128, B, T, E])
        pair_gt = sb("pair_gt", [128, T * E * E])
        pair_eq = sb("pair_eq", [128, T * E * E])
        rank = sb("rank", [128, T * E])
        cw = sb("cw", [128, T, E])
        mx = sb("mx", [128, 2, T])
        wT = sb("wT", [E, B, S])
        wb = sb("wb", [128, E, CH])
        gate = P[:, 3, 0:2 * CH].rearrange("p (a b) -> p a b", a=2)
        sig = P[:, 3, 2 * CH:4 * CH].rearrange("p (a b) -> p a b", a=2)
        up = sb("up", [128, 2, CH])
        aw = sb("aw", [128, 2, CH])
        UP = [up[:, 0, :], up[:, 1, :], pair_gt[:, :]]
        AW = [aw[:, 0, :], aw[:, 1, :], pair_eq[:, :]]
        yT = sb("yT", [128, CH])
        ys = sb("ys", [128, T, D])
        gu_scaled = wb[:, :, :]
        staging = P[:, :, :].rearrange("p a b -> p (a b)")
        gu_in = staging[:, 0:4 * E * 128].rearrange("p (m d) -> p m d", d=128)
        dn_in = staging[:, 4 * E * 128:6 * E * 128].rearrange("p (e i) -> p e i", i=I)

        ps = ctx.enter_context(nc.psum_tensor("ps", [128, 4096], fp32))

        def bank(i, n=1):
            return ps[:, i * 512:(i + n) * 512]

        PAIR = [bank(0, 2), bank(4, 2)]
        OB = [bank(2), bank(6)]
        M = bank(3)
        SIDE = bank(7)
        LS = [bank(0), bank(1)]
        LO = bank(2)
        RING = [bank(4), bank(5), bank(6)]
        Y = bank(7)

        def q_banks(qh):
            if qh == 0:
                return [bank(0), bank(1), bank(2), bank(3), bank(0), bank(1), bank(2)]
            return [SIDE if qh < 6 else bank(1)] * 7

        w_dram = nc.dram_tensor("combine_rows", [B, E, S], fp32, kind="Internal").ap()

        s_prep = sem("projection_weights_loaded")
        s_att = sem("attn_weights_loaded")
        s_gw = [sem(f"gate_up_weights_loaded_{i}") for i in range(E // 2)]
        s_ffn = sem("ffn_inputs_loaded")
        s_zero = sem("pads_written")
        s_pw = sem("prep_product")
        s_pe_ = sem("prep_evacuated")
        s_tp = sem("ffn_weight_transposed")
        s_te = sem("ffn_weight_hi_written")
        s_tl = sem("ffn_weight_lo_written")
        s_x = [sem(f"x_loaded_{i}") for i in range(2 * B)]
        s_link = sem("vector_step")
        s_plink = sem("pool_step")
        s_xn = sem("normed")
        s_xtp = sem("x_transposed")
        s_xts = sem("xT_written")
        s_xh = sem("x_hi_written")
        s_xl = sem("x_lo_written")
        s_prj = sem("projected")
        s_pev = sem("projection_evacuated")
        s_sq = sem("squares_done")
        s_cos = sem("rope_cos_done")
        s_sin = sem("rope_sin_done")
        s_rot = sem("rotated")
        s_stk = sem("parts_stacked")
        s_kt = sem("k_transposed")
        s_kTs = sem("kT_written")
        s_qt = sem("q_transposed")
        s_qTs = sem("qT_written")
        s_lg = sem("logits_done")
        s_lgs = sem("logits_written")
        s_lx = sem("logits_shifted")
        s_le = sem("logits_exp")
        s_cw = sem("combine_done")
        s_wtp = sem("combine_transposed")
        s_wts = sem("wT_written")
        s_wst = sem("combine_stored")
        s_wb = [sem(f"combine_broadcast_{i}") for i in range(2)]
        s_sc = sem("scores_done")
        s_ex = sem("exp_done")
        s_mk = sem("masked")
        s_pv = sem("pv_done")
        s_lsc = sem("local_scores_done")
        s_lex = sem("local_exp_done")
        s_lmk = sem("local_masked")
        s_lpv = sem("local_pv_done")
        s_o = sem("o_evacuated")
        s_ot = sem("o_transposed")
        s_on = sem("o_normalised")
        s_ont = sem("on_transposed")
        s_ons = sem("onT_written")
        s_wo = sem("wo_done")
        s_x1 = sem("residual_added")
        s_g = sem("gate_done")
        s_u = sem("up_done")
        s_gs = sem("gate_evacuated")
        s_gm = sem("gate_limited")
        s_th = sem("tanh_done")
        s_us = sem("up_evacuated")
        s_a = sem("act_done")
        s_aw = sem("act_weighted")
        s_dn = sem("down_done")
        s_ys = sem("y_evacuated")
        s_yt = sem("y_transposed")
        s_yth = sem("y_tanh")
        s_yd = sem("y_times_tanh")
        s_out = sem("result_ready")
        s_st = sem("result_stored")

        block = ctx.enter_context(nc.Block())

        @block.sync
        def _(sp):
            def load_x(b, h):
                sp.dma_start(xs[:, b, h * HT:(h + 1) * HT, :],
                             hidden[b, h * HT * 128:(h + 1) * HT * 128, :].rearrange("(t p) d -> p t d", p=128)).then_inc(s_x[2 * b + h], 16)

            load_x(0, 0)
            for dst, src in ((kvd[:, :], g_kvd), (k32[:, :], c32), (kvu[:, 0:32], g_ku), (kvu[:, 32:64], g_vu),
                             (norm_w["g"][:, :], n1.rearrange("(p o) -> p o", o=1)), (wq_in["g"][:, :], g_wq),
                             (rw_in[:, :], r_w), (rb[:, :], r_b.rearrange("(o e) -> o e", o=1).to_broadcast([128, E]))):
                sp.dma_start(dst, src).then_inc(s_prep, 16)
            load_x(0, 1)
            for i in range(E // 2):
                sp.dma_start(gu_in[:, 8 * i:8 * i + 8, :], gu_w[2 * i:2 * i + 2, :, :].rearrange("e (m j) d -> j (e m) d", j=128)) \
                    .then_inc(s_gw[i], 16)
            for dst, src in ((gub_in[:, :], gu_b.rearrange("e (m j) -> (e m) j", j=128)), (dnb[:, :], dn_b),
                             (dn_in, dn_w.rearrange("e d i -> d e i"))):
                sp.dma_start(dst, src).then_inc(s_ffn, 16)
            for dst, src in ((k16[:, :], c16), (norm_w["l"][:, :], n2.rearrange("(p o) -> p o", o=1)), (wo["g"][:, :], g_wo),
                             (wq_in["l"][:, :], l_wq), (wkv_in[:, 0:32], l_wk), (wkv_in[:, 32:64], l_wv), (wo["l"][:, :], l_wo)):
                sp.dma_start(dst, src).then_inc(s_att, 16)
            for b in range(1, B):
                for h in range(2):
                    load_x(b, h)
            for g in range(B * NCH):
                b, c = divmod(g, NCH)
                if c == 0:
                    sp.wait_ge(s_wts, 2 * (b + 1))
                    sp.dma_start(w_dram[b, :, :], wT[:, b, :]).then_inc(s_wst, 16)
                    sp.wait_ge(s_wst, 16 * (b + 1))
                for half in range(2):
                    if g == 0:
                        sp.wait_ge(s_tl, NGUW)
                    else:
                        sp.wait_ge(s_aw, (g - 1) * E * IT + (half + 1) * E * IT // 2)
                    es = slice(half * E // 2, (half + 1) * E // 2)
                    sp.dma_start(wb[:, es, :], w_dram[b, es, c * CH:(c + 1) * CH].rearrange("(o e) s -> o e s", o=1)
                                 .to_broadcast([128, E // 2, CH])).then_inc(s_wb[half], 16)
                done = [g - NCH, g - NCH + 1] if c == 0 and g > 0 else [g - 1, g] if g == B * NCH - 1 else []
                for r in done:
                    sp.wait_ge(s_out, r + 1)
                    rb_, rc = divmod(r, NCH)
                    sp.dma_start(out[rb_, rc * CH:(rc + 1) * CH, :].rearrange("(t p) d -> p t d", p=128),
                                 ys[:, rc * CH // 128:(rc + 1) * CH // 128, :]).then_inc(s_st, 16)
            sp.wait_ge(s_st, B * NCH * 16)

        @block.tensor
        def _(pe):
            pe.wait_ge(s_prep, 8 * 16)
            nc.tensor.transpose(SIDE[0:32, 0:128], kvd[:, :], ident).then_inc(s_pw, 1)
            nc.tensor.transpose(SIDE[:, 192:192 + E], rw_in[:, :], ident[0:E, 0:E]).then_inc(s_pw, 1)

            def first_weights():
                pe.wait_ge(s_pe_, 2)
                nc.tensor.matmul(SIDE[:, 128:192], kvdT[:, :], kvu[:, :], start=True, stop=True).then_inc(s_pw, 1)

            def weights(n):
                if n < NGUW:
                    pe.wait_ge(s_gw[n // 2], 16)
                if n == NGUW:
                    pe.wait_ge(s_ffn, 3 * 16)
                    pe.wait_ge(s_pe_, 4)
                    nc.tensor.transpose(SIDE[:, 256:256 + 4 * E], gub_in[:, :], ident[0:4 * E, 0:4 * E]).then_inc(s_pw, 1)
                if n >= NW:
                    return
                if n >= 3:
                    pe.wait_ge(s_te, n - 2)
                for i in range(4):
                    m = 4 * n + i
                    src = gu_in[:, m, :] if m < 4 * E else dn_in[:, (m - 4 * E) // IT, ((m - 4 * E) % IT) * 128:((m - 4 * E) % IT + 1) * 128]
                    last = nc.tensor.transpose(RING[n % 3][:, i * 128:(i + 1) * 128], src, ident)
                last.then_inc(s_tp, 1)

            def qkv(qh, k):
                q, h = divmod(qh, 2)
                b, ph = STAGES[q]
                XT, PR0, PR1, LG, KT, QT0, QT1 = q_banks(qh)
                if k == "xT":
                    if ph == "g":
                        pe.wait_ge(s_xn, qh + 1)
                    else:
                        pe.wait_ge(s_x1, b * T + (h + 1) * HT)
                    if qh > 0:
                        pe.wait_ge(s_qTs, 2 * qh)
                    if qh == 1:
                        pe.wait_ge(s_pe_, 6)
                    if qh == 4:
                        pe.wait_ge(s_wts, 2)
                    if qh == 6:
                        pe.wait_ge(s_ex, 2 * NU)
                    for i in range(HT):
                        last = nc.tensor.transpose(XT[:, i * 128:(i + 1) * 128], x[:, b, h * HT + i, :], ident)
                    last.then_inc(s_xtp, 1)
                if k in ("project0", "project1"):
                    i = int(k[-1])
                    if i == 0:
                        pe.wait_ge(s_xts, qh + 1)
                        if qh == 0:
                            pe.wait_ge(s_pe_, 4)
                        if qh == 4:
                            pe.wait_ge(s_pe_, 7)
                    elif qh > 0:
                        pe.wait_ge(s_pev, 2 * qh + 1)
                    for j in range(2):
                        last = nc.tensor.matmul((PR0, PR1)[i][:, j * PROJ:(j + 1) * PROJ], xT[:, (2 * i + j) * 128:(2 * i + j + 1) * 128],
                                                wproj[ph][:, :], start=True, stop=True)
                    last.then_inc(s_prj, 1)
                if k == "logits" and ph == "g":
                    if qh > 0:
                        pe.wait_ge(s_pev, 2 * qh + 2)
                    for i in range(HT):
                        last = nc.tensor.matmul(LG[:, i * E:(i + 1) * E], xT[:, i * 128:(i + 1) * 128], rwT[:, :],
                                                start=True, stop=True)
                    last.then_inc(s_lg, 1)

                def turn(dst, t, head):
                    return nc.tensor.transpose(dst, stk[:, t * HEADS + head:t * HEADS + head + KVH, :, :].rearrange("p a b d -> p (a b d)"),
                                               k16[:, :])

                if k == "kT":
                    pe.wait_ge(s_stk, qh + 1)
                    if qh == 0:
                        pe.wait_ge(s_att, 7 * 16)
                    for t in range(HT):
                        last = turn(KT.bitcast(fp16)[:, t * 128:(t + 1) * 128], t, H)
                    last.then_inc(s_kt, 1)
                if k in ("qT0", "qT1"):
                    i = int(k[-1])
                    if qh > 0:
                        pe.wait_ge(*((s_kTs, qh + 1) if i == 0 else (s_qTs, 2 * qh + 1)))
                    for a in range(2):
                        for j in range(J):
                            at = a * 512 + j * 128
                            last = turn((QT0, QT1)[i].bitcast(fp16)[:, at:at + 128], 2 * i + a, j * KVH)
                    last.then_inc(s_qt, 1)

            def router(b, k):
                if k in ("wT0", "wT1"):
                    i = int(k[-1])
                    if i == 0:
                        pe.wait_ge(s_cw, b + 1)
                        pe.wait_ge(s_qTs, 8 + 4 * b)
                    else:
                        pe.wait_ge(s_wts, 2 * b + 1)
                    for j in range(HT):
                        last = nc.tensor.transpose(SIDE[0:E, j * 128:(j + 1) * 128], cw[:, i * HT + j, :], ident)
                    last.then_inc(s_wtp, 1)

            def scores(u, part):
                b, t, kt = UNITS[u]
                if kt == t and t in (0, HT) and part == 0:
                    pe.wait_ge(s_kTs, 2 * b + 1 + t // HT)
                if kt == t and t % 2 == 0 and part == 0:
                    pe.wait_ge(s_qTs, 4 * b + t // 2 + 1)
                if u == 0 and part == 1:
                    pe.wait_ge(s_te, NW)
                if u > 0:
                    pe.wait_ge(s_ex, 2 * u + part - 1)
                for c in (2 * part, 2 * part + 1):
                    last = nc.tensor.matmul(PAIR[part][:, (c % 2) * 512:(c % 2 + 1) * 512], kz[:, b, c, kt * 128:(kt + 1) * 128],
                                            qT[:, b, t, :], start=True, stop=True)
                last.then_inc(s_sc, 1)

            def pv(u):
                b, t, kt = UNITS[u]
                p = b * T + t
                first = kt == t
                if first and p >= 2:
                    pe.wait_ge(s_o, p - 1)
                pe.wait_ge(s_ex, 2 * u + 2)
                if first:
                    pe.wait_ge(s_mk, 2 * p + 2)
                for c in range(KVH):
                    last = nc.tensor.matmul(OB[p % 2][32 * c:32 * c + 32, :], v[:, b, kt, c, :], P[:, u % 4, c * 512:(c + 1) * 512],
                                            start=first, stop=u in ENDS)
                last.then_inc(s_pv, 1)

            def o_transpose(p):
                if p > 0:
                    pe.wait_ge(s_x1, p)
                pe.wait_ge(s_o, p + 1)
                for j in range(J):
                    last = nc.tensor.transpose(M[:, j * 128:(j + 1) * 128], oT[:, p % 3, j * 128:(j + 1) * 128], ident)
                last.then_inc(s_ot, 1)

            def on_transpose(p):
                pe.wait_ge(s_on, p + 1)
                nc.tensor.transpose(M[:, 0:128], on[:, p % 2, :], ident).then_inc(s_ont, 1)

            def project_out(p):
                pe.wait_ge(s_ons, p + 1)
                nc.tensor.matmul(M[:, 128:256], onT[:, p % 2, :], wo["g" if p < B * T else "l"][:, :], start=True, stop=True).then_inc(s_wo, 1)

            def global_step(u):
                if u - 2 * LAG in TURNS:
                    project_out(TURNS[u - 2 * LAG])
                if u + 1 < NU:
                    scores(u + 1, 0)
                if u - LAG in TURNS:
                    on_transpose(TURNS[u - LAG])
                if 0 <= u - 2 < NU:
                    pv(u - 2)
                if u in TURNS:
                    o_transpose(TURNS[u])
                if u + 1 < NU:
                    scores(u + 1, 1)

            def local_scores(lt, k):
                b, t = divmod(lt, T)
                n = b * LJ + local_job(t, k)
                if n == 0:
                    pe.wait_ge(s_ex, 2 * NU)
                else:
                    pe.wait_ge(s_lex, n if b == 0 else n - 1)
                if b > 0 and t == 0 and k == 0:
                    pe.wait_ge(s_qTs, 16)
                s = LS[n % 2 if b else 0]
                if k == 0 and t in (0, HT):
                    qh = 2 * (B + b) + t // HT
                    pe.wait_ge(s_kTs, qh + 1)
                    pe.wait_ge(s_qTs, 2 * qh + 2)
                if k < 4:
                    last = nc.tensor.matmul(s, kz[:, b, k, t * 128:(t + 1) * 128], qT[:, b, t, :], start=True, stop=True)
                else:
                    qs = qT[:, b, t, :].rearrange("p (j q) -> p j q", q=128)[:, :, 0:WIN]
                    for c in range(KVH):
                        last = nc.tensor.matmul(s[128 - WIN:128, c * 128:(c + 1) * 128], kz[:, b, c, t * 128 - WIN:t * 128], qs,
                                                start=True, stop=True)
                last.then_inc(s_lsc, 1)

            def local_pv(lt):
                b, t = divmod(lt, T)
                pe.wait_ge(s_o, B * T + lt)
                pe.wait_ge(s_lmk, b * LJ + local_job(t, 4 if t else 3) + 1)
                for c in range(KVH):
                    last = nc.tensor.matmul(LO[32 * c:32 * c + 32, :], v[:, b, t, c, :], P[:, lt % 3, c * 512:(c + 1) * 512],
                                            start=True, stop=t == 0)
                if t > 0:
                    for c in range(KVH):
                        last = nc.tensor.matmul(LO[32 * c:32 * c + 32, :].rearrange("p (j q) -> p j q", q=128)[:, :, 0:WIN],
                                                v[:, b, t - 1, c, :], Pp[:, lt % 2, c * 128:(c + 1) * 128], start=False, stop=True)
                last.then_inc(s_lpv, 1)

            def local_step(lt, k):
                if lt < B * T and (k < 4 or lt % T):
                    local_scores(lt, k)
                p = B * T + lt - 1
                if 2 <= lt and k == 1:
                    project_out(p - 1)
                if 1 <= lt <= B * T:
                    if k == 1:
                        local_pv(lt - 1)
                    if k == 2:
                        o_transpose(p)
                    if k == 4:
                        on_transpose(p)

            def ffn(n, part):
                g, r = divmod(n, E * IT)
                e, i = divmod(r, IT)
                b, x0 = g // NCH, (g % NCH) * CH

                def hidden(quarter, m, done):
                    if m >= 3:
                        pe.wait_ge(s_gs if (m - 3) % 2 == 0 else s_us, (m - 3) // 2 + 1)
                    for w, src in ((guh, xh), (guh, xl), (gul, xh)):
                        last = nc.tensor.matmul(RING[m % 3], w[:, 4 * e + quarter, :], src[:, b, x0:x0 + CH],
                                                start=(w, src) == (guh, xh), stop=w is gul)
                    last.then_inc(done, 1)

                if n == 0 and part == 0:
                    pe.wait_ge(s_ex, 2 * NU)
                    pe.wait_ge(s_tl, NGUW)
                if n % HU == 0 and n < B * HU and part == 0:
                    pe.wait_ge(s_xl, 2 * b + 2)
                    pe.wait_ge(s_xh, 2 * b + 2)
                if n < B * HU and part == 0:
                    if n == 1:
                        pe.wait_ge(s_o, B * T)
                    hidden(i, 2 * n, s_g)
                if n < B * HU and part == 1:
                    hidden(IT + i, 2 * n + 1, s_u)
                if n >= DOWN_LAG and part == 1:
                    m = n - DOWN_LAG
                    g, r = divmod(m, E * IT)
                    if r == 0 and g > 0:
                        pe.wait_ge(s_yd, g)
                    if m == 0:
                        pe.wait_ge(s_qTs, 12)
                        pe.wait_ge(s_wts, 4)
                    if r == 0:
                        c = g % NCH
                        nc.tensor.matmul(Y, dnb[:, :], wT[:, g // NCH, c * CH:(c + 1) * CH], start=True, stop=False)
                    pe.wait_ge(s_aw, m + 1)
                    nc.tensor.matmul(Y, dnT[:, r, :], AW[m % 3], start=False, stop=r == E * IT - 1).then_inc(s_dn, 1)

            def y_back(g, k):
                if k == 1:
                    pe.wait_ge(s_ys, g + 1)
                    for i in range(CH // 128):
                        last = nc.tensor.transpose(Y[:, i * 128:(i + 1) * 128], yT[:, i * 128:(i + 1) * 128], ident)
                    last.then_inc(s_yt, 1)

            steps = {"P": first_weights, "Q": qkv, "R": router, "G": global_step, "L": local_step, "F": ffn, "Y": y_back, "W": weights}
            for kind, *args in SCHEDULE:
                if kind in steps:
                    steps[kind](*args)

        @block.scalar
        def _(act):
            def weights(n):
                if n >= NW:
                    return
                act.wait_ge(s_tp, n + 1)
                if n < NGUW:
                    nc.scalar.activation(gu_scaled[:, n, :], RING[n % 3], ACT.Copy, scale=WSCALE)
                    nc.scalar.activation(guh[:, 4 * n:4 * n + 4, :].rearrange("p a b -> p (a b)"), RING[n % 3], ACT.Copy,
                                         scale=WSCALE).then_inc(s_te, 1)
                else:
                    m = 4 * (n - NGUW)
                    nc.scalar.activation(dnT[:, m:m + 4, :].rearrange("p a b -> p (a b)"), RING[n % 3], ACT.Copy,
                                         scale=0.5).then_inc(s_te, 1)

            def qkv(qh, k):
                q, h = divmod(qh, 2)
                b, ph = STAGES[q]
                banks = q_banks(qh)
                if k == "xT":
                    if qh in BETWEEN:
                        return
                    act.wait_ge(s_xtp, qh + 1)
                    if qh > 0:
                        act.wait_ge(s_prj, 2 * qh)
                        act.wait_ge(s_lg, min(qh, 2 * B))
                        act.wait_ge(s_xl, min(qh, 2 * B))
                    nc.scalar.activation(xT[:, :], banks[0], ACT.Copy).then_inc(s_xts, 1)
                if k == "project0" and ph == "g":
                    act.wait_ge(s_xts, qh + 1)
                    nc.scalar.activation(xh[:, b, h * HT * 128:(h + 1) * HT * 128], xT[:, :], ACT.Copy, scale=WSCALE).then_inc(s_xh, 1)
                if k in ("qT0", "qT1") and qh not in BETWEEN:
                    i = int(k[-1])
                    act.wait_ge(s_qt, 2 * qh + i + 1)
                    if qh == 6:
                        act.wait_ge(s_pv, NU)
                    t = h * HT + 2 * i
                    nc.scalar.activation(qT[:, b, t:t + 2, :].rearrange("p a b -> p (a b)"), banks[5 + i].bitcast(fp16),
                                         ACT.Copy).then_inc(s_qTs, 1)

            def router(b, k):
                if k == "rank":
                    act.wait_ge(s_lx, b + 1)
                    if b > 0:
                        act.wait_ge(s_wts, 2 * b)
                    nc.scalar.activation(cw[:, :, :], lg[:, b, :, :], ACT.Exp).then_inc(s_le, 1)

            def global_step(u):
                if 0 <= u < NU:
                    for part in range(2):
                        act.wait_ge(s_sc, 2 * u + part + 1)
                        if part == 0 and u >= 4:
                            act.wait_ge(s_pv, u - 3)
                        nc.scalar.activation(P[:, u % 4, part * 1024:(part + 1) * 1024], PAIR[part], ACT.Exp,
                                             scale=EXP_SCALE).then_inc(s_ex, 1)

            def local_step(lt, k):
                if lt < B * T and (k < 4 or lt % T):
                    b, t = divmod(lt, T)
                    if lt == 0 and k == 0:
                        act.wait_ge(s_pv, NU)
                    if lt >= 3 and k == 0:
                        act.wait_ge(s_lpv, lt - 2)
                    n = b * LJ + local_job(t, k)
                    s = LS[n % 2 if b else 0]
                    act.wait_ge(s_lsc, n + 1)
                    if k < 4:
                        nc.scalar.activation(P[:, lt % 3, k * 512:(k + 1) * 512], s, ACT.Exp, scale=EXP_SCALE).then_inc(s_lex, 1)
                    else:
                        nc.scalar.activation(Pp[128 - WIN:128, lt % 2, :], s[128 - WIN:128, :], ACT.Exp,
                                             scale=EXP_SCALE).then_inc(s_lex, 1)
                if 1 <= lt <= B * T and k == 1:
                    p = B * T + lt - 1
                    act.wait_ge(s_lpv, lt)
                    act.wait_ge(s_ot, p - 1)
                    nc.scalar.activation(oT[:, p % 3, :], LO, ACT.Copy).then_inc(s_o, 1)

            def ffn(n, part):
                e, i = (n // IT) % E, n % IT
                if part == 0 and 1 <= n <= B * HU:
                    m = n - 1
                    act.wait_ge(s_gm, m + 1)
                    nc.scalar.activation(sig[:, m % 2, :], gate[:, m % 2, :], ACT.Tanh, scale=ALPHA / 2).then_inc(s_th, 1)
                if n >= B * HU:
                    return
                if part == 0:
                    act.wait_ge(s_g, n + 1)
                    if n == 0:
                        act.wait_ge(s_pv, NU)
                    if n >= 2:
                        act.wait_ge(s_a, n - 1)
                    nc.scalar.activation(gate[:, n % 2, :], RING[(2 * n) % 3], ACT.Identity, scale=1.0 / ACC,
                                         bias=gub[:, e, i:i + 1]).then_inc(s_gs, 1)
                else:
                    act.wait_ge(s_u, n + 1)
                    if n == 2:
                        act.wait_ge(s_cw, B)
                    if n >= 3:
                        act.wait_ge(s_aw, n - 2)
                    nc.scalar.activation(UP[n % 3], RING[(2 * n + 1) % 3], ACT.Identity, scale=1.0 / ACC,
                                         bias=gub[:, e, IT + i:IT + i + 1]).then_inc(s_us, 1)

            def y_back(g, k):
                if k == 0:
                    act.wait_ge(s_dn, (g + 1) * E * IT)
                    nc.scalar.activation(yT[:, :], Y, ACT.Copy).then_inc(s_ys, 1)
                else:
                    c = g % NCH
                    act.wait_ge(s_yt, g + 1)
                    if c == 0 and g > 0:
                        act.wait_ge(s_st, g * 16)
                    nc.scalar.activation(ys[:, c * CH // 128:(c + 1) * CH // 128, :].rearrange("p t d -> p (t d)"), Y, ACT.Tanh,
                                         scale=0.5).then_inc(s_yth, 1)

            steps = {"Q": qkv, "R": router, "G": global_step, "L": local_step, "F": ffn, "Y": y_back, "W": weights}
            for kind, *args in SCHEDULE:
                if kind in steps:
                    steps[kind](*args)

        @block.gpsimd
        def _(pool):
            linked = [0]

            def link(ins):
                ins.then_inc(s_plink, 1)
                linked[0] += 1
                pool.wait_ge(s_plink, linked[0])

            nc.gpsimd.memset(kz[:, 0, :, :].bitcast(fp32), 0.0).then_inc(s_zero, 1)
            link(nc.gpsimd.memset(v[:, 0, :, :, :], 0.0))
            nc.gpsimd.memset(v[:, 0, :, :, HD:HD + 1], 1.0).then_inc(s_zero, 1)
            nc.gpsimd.memset(kz[:, 1, :, :].bitcast(fp32), 0.0).then_inc(s_zero, 1)
            link(nc.gpsimd.memset(v[:, 1, :, :, :], 0.0))
            nc.gpsimd.memset(v[:, 1, :, :, HD:HD + 1], 1.0).then_inc(s_zero, 1)
            nc.gpsimd.memset(Pp[:, :, :], 0.0).then_inc(s_zero, 1)

            def qkv(qh, k):
                h, ph = qh % 2, STAGES[qh // 2][1]
                if k == "project1":
                    pool.wait_ge(s_pev, 2 * qh + 2)
                    if qh > 0:
                        pool.wait_ge(s_stk, qh)
                    nc.gpsimd.tensor_tensor(sq[:, :, :], qk[:, :, :], qk[:, :, :], ALU.mult).then_inc(s_sq, 1)
                    heads = lambda a: a[:, :, :].rearrange("p (t h) d -> p t h d", t=HT)
                    cos = rope[ph][:, h * HT * HD:(h + 1) * HT * HD].rearrange("p (t o d) -> p t o d", t=HT, o=1) \
                        .to_broadcast([128, HT, HEADS, HD])
                    nc.gpsimd.tensor_tensor(heads(rot), heads(qk), cos, ALU.mult).then_inc(s_cos, 1)
                if k == "rope":
                    pool.wait_ge(s_cos, qh + 1)
                    pool.wait_ge(s_sin, qh + 1)
                    nc.gpsimd.tensor_tensor(rot[:, :, :], rot[:, :, :], rtmp[:, :, :], ALU.add).then_inc(s_rot, 1)

            def global_step(u):
                if 0 <= u < NU and UNITS[u][1] == UNITS[u][2]:
                    for part in range(2):
                        pool.wait_ge(s_ex, 2 * u + part + 1)
                        p = P[:, u % 4, part * 1024:(part + 1) * 1024].rearrange("p (h q) -> p h q", q=128)
                        nc.gpsimd.affine_select(out=p, in_=p, compare_op=ALU.is_ge, fill=0.0, base=0,
                                                pattern=[[0, 8], [1, 128]], channel_multiplier=-1).then_inc(s_mk, 1)

            def local_step(lt, k):
                if lt < B * T and (k < 4 or lt % T):
                    b, t = divmod(lt, T)
                    pool.wait_ge(s_lex, b * LJ + local_job(t, k) + 1)
                    if k < 4:
                        p = P[:, lt % 3, k * 512:(k + 1) * 512].rearrange("p (h q) -> p h q", q=128)
                        link(nc.gpsimd.affine_select(out=p, in_=p, compare_op=ALU.is_ge, fill=0.0, base=0,
                                                     pattern=[[0, J], [1, 128]], channel_multiplier=-1))
                        late = p[:, :, WIN:128]
                        nc.gpsimd.affine_select(out=late, in_=late, compare_op=ALU.is_ge, fill=0.0, base=-1,
                                                pattern=[[0, J], [-1, 128 - WIN]], channel_multiplier=1).then_inc(s_lmk, 1)
                    else:
                        p = Pp[:, lt % 2, :].rearrange("p (h q) -> p h q", q=WIN)
                        nc.gpsimd.affine_select(out=p, in_=p, compare_op=ALU.is_ge, fill=0.0, base=WIN - 129,
                                                pattern=[[0, H], [-1, WIN]], channel_multiplier=1).then_inc(s_lmk, 1)

            def ffn(n, part):
                if part == 1 and 1 <= n <= B * HU:
                    m = n - 1
                    g, r = divmod(m, E * IT)
                    e = r // IT
                    if r % (E * IT // 2) == 0:
                        pool.wait_ge(s_wb[2 * r // (E * IT)], 16 * (g + 1))
                    pool.wait_ge(s_a, m + 1)
                    if m >= 3:
                        pool.wait_ge(s_dn, m - 2)
                    nc.gpsimd.tensor_tensor(AW[m % 3], UP[m % 3], wb[:, e, :], ALU.mult).then_inc(s_aw, 1)

            def low_weights(n):
                pool.wait_ge(s_te, n + 1)
                nc.gpsimd.tensor_tensor(gul[:, 4 * n:4 * n + 4, :].rearrange("p a b -> p (a b)"), gu_scaled[:, n, :],
                                        guh[:, 4 * n:4 * n + 4, :].rearrange("p a b -> p (a b)"), ALU.subtract).then_inc(s_tl, 1)

            steps = {"Q": qkv, "G": global_step, "L": local_step, "F": ffn, "V": low_weights}
            for kind, *args in SCHEDULE:
                if kind in steps:
                    steps[kind](*args)

        @block.vector
        def _(dve):
            linked = [0]

            def link(ins):
                ins.then_inc(s_link, 1)
                linked[0] += 1
                dve.wait_ge(s_link, linked[0])

            def rsqrt(y, x, n, newton=(0, 1, 2)):
                t0, t1 = ntmp[:, 0, 0:n], ntmp[:, 1, 0:n]
                if 0 in newton:
                    link(nc.vector.tensor_scalar(y.bitcast(i32), x.bitcast(i32), -0.5, MAGIC, ALU.mult, ALU.add))
                for _ in newton:
                    link(nc.vector.scalar_tensor_tensor(t0, y, -0.5, y, ALU.mult, ALU.mult))
                    link(nc.vector.tensor_tensor(t1, t0, x, ALU.mult))
                    link(nc.vector.scalar_tensor_tensor(y, t1, 1.5, y, ALU.add, ALU.mult))

            def bcast(ap, n):
                m = ap.shape[1]
                return ap.rearrange("p (m o) -> p m o", o=1).to_broadcast([128, m, n])

            def projection_weights(ph):
                return nc.vector.tensor_scalar(wproj[ph][:, 0:H * HD].rearrange("p (j c d) -> p j c d", j=J, c=KVH),
                                               wq_in[ph][:, :].rearrange("p (c j d) -> p j c d", j=J, c=KVH),
                                               norm_w[ph][:, 0:1], None, ALU.mult)

            def weights(n):
                if n == NW:
                    dve.wait_ge(s_pw, 4)
                    bT = SIDE[:, 256:256 + 4 * E].rearrange("p (e m) -> p e m", m=4)
                    nc.vector.tensor_copy(gub[:, :, 0:IT], bT[:, :, 0:IT]).then_inc(s_pe_, 1)
                    nc.vector.tensor_scalar(gub[:, :, IT:2 * IT], bT[:, :, IT:2 * IT], 1.0, None, ALU.add).then_inc(s_pe_, 1)
                    dve.wait_ge(s_att, 7 * 16)
                    projection_weights("l")
                    nc.vector.tensor_scalar(wproj["l"][:, H * HD:PROJ], wkv_in[:, :], norm_w["l"][:, 0:1], None, ALU.mult) \
                        .then_inc(s_pe_, 1)

            def qkv(qh, k):
                q, h = divmod(qh, 2)
                b, ph = STAGES[q]
                banks = q_banks(qh)
                ts = range(h * HT, (h + 1) * HT)
                if k == "stats" and ph == "g":
                    dve.wait_ge(s_x[qh], 16)
                    for i, t in enumerate(ts):
                        last = nc.vector.bn_stats(stats[:, i, :], xs[:, b, t, :])
                    link(last)
                    for i in range(HT):
                        last = nc.vector.bn_aggr(mv[:, i, :], stats[:, i, :])
                    link(last)
                    link(nc.vector.tensor_scalar(rs[:, qh % 2, 2, :], mv[:, :, 1], LN_EPS, None, ALU.add))
                    link(nc.vector.reciprocal(rs[:, qh % 2, 3, :], rs[:, qh % 2, 2, :]))
                    link(nc.vector.tensor_tensor(rs[:, qh % 2, 3, :], rs[:, qh % 2, 3, :], mv[:, :, 1], ALU.mult))
                    link(nc.vector.tensor_scalar(rs[:, qh % 2, 3, :], rs[:, qh % 2, 3, :], RMS_EPS, None, ALU.add))
                if k == "std" and ph == "g":
                    rsqrt(rs[:, qh % 2, 0:2, :].rearrange("p a t -> p (a t)"), rs[:, qh % 2, 2:4, :].rearrange("p a t -> p (a t)"), 2 * HT)
                if k == "norm" and ph == "g":
                    for i, t in enumerate(ts):
                        last = nc.vector.tensor_scalar(x[:, b, t, :], xs[:, b, t, :], mv[:, i, 0:1], rs[:, qh % 2, 0, i:i + 1],
                                                       ALU.subtract, ALU.mult)
                    last.then_inc(s_xn, 1)
                if k == "stats" and ph == "l":
                    s4 = xsq[:, :, :]
                    xx = x[:, b, h * HT:(h + 1) * HT, :]
                    dve.wait_ge(s_x1, b * T + (h + 1) * HT)
                    link(nc.vector.tensor_tensor(s4, xx, xx, ALU.mult))
                    link(nc.vector.tensor_reduce(rs[:, qh % 2, 2, :], s4, AXX, ALU.add))
                    link(nc.vector.tensor_scalar(rs[:, qh % 2, 3, :], rs[:, qh % 2, 2, :], 1.0 / D, RMS_EPS, ALU.mult, ALU.add))
                if k == "std" and ph == "l":
                    rsqrt(rs[:, qh % 2, 1, :], rs[:, qh % 2, 3, :], HT)
                if k == "xT" and qh in BETWEEN:
                    dve.wait_ge(s_xtp, qh + 1)
                    dve.wait_ge(s_prj, 2 * qh)
                    dve.wait_ge(s_lg, min(qh, 2 * B))
                    dve.wait_ge(s_xh, min(qh, 2 * B))
                    dve.wait_ge(s_xl, min(qh, 2 * B))
                    nc.vector.tensor_copy(xT[:, :], banks[0]).then_inc(s_xts, 1)
                if k in ("project0", "project1"):
                    i = int(k[-1])
                    if qh == 0:
                        dve.wait_ge(s_zero, 5)
                    if ph == "l" and h == 0:
                        dve.wait_ge(s_pv, (b + 1) * NG)
                    dve.wait_ge(s_prj, 2 * qh + i + 1)
                    src = banks[1 + i][:, 0:2 * PROJ].rearrange("p (t n) -> p t n", t=2)
                    r = rs[:, qh % 2, 1, 2 * i:2 * i + 2]
                    t = h * HT + 2 * i
                    nc.vector.tensor_tensor(qk[:, 2 * i * HEADS:(2 * i + 2) * HEADS, :].rearrange("p (t a) d -> p t (a d)", t=2),
                                            src[:, :, 0:QK], bcast(r, QK), ALU.mult)
                    nc.vector.tensor_tensor(v[:, b, t:t + 2, :, 0:HD], src[:, :, QK:PROJ].rearrange("p t (c d) -> p t c d", c=KVH),
                                            r.rearrange("p (t o q) -> p t o q", o=1, q=1).to_broadcast([128, 2, KVH, HD]), ALU.mult) \
                        .then_inc(s_pev, 1)
                if k == "rope":
                    if qh > 0:
                        dve.wait_ge(s_rot, qh)
                    dve.wait_ge(s_pev, 2 * qh + 2)
                    sin = rope[ph][:, (T + h * HT) * HD:(T + (h + 1) * HT) * HD].rearrange("p (t o d w) -> p t o d w", t=HT, o=1, w=2)
                    q5 = qk[:, :, :].rearrange("p (t h) (d w) -> p t h d w", t=HT, w=2)
                    r5 = rtmp[:, :, :].rearrange("p (t h) (d w) -> p t h d w", t=HT, w=2)
                    for w in range(2):
                        last = nc.vector.tensor_tensor(r5[:, :, :, :, w], q5[:, :, :, :, 1 - w],
                                                       sin[:, :, :, :, w].to_broadcast([128, HT, HEADS, HD // 2]), ALU.mult)
                    last.then_inc(s_sin, 1)
                    dve.wait_ge(s_sq, qh + 1)
                    link(nc.vector.tensor_reduce(msq[:, :], sq[:, :, :], AXX, ALU.add))
                if k == "newton1":
                    c = 1.0 / (QKSCALE * QKSCALE)
                    link(nc.vector.tensor_scalar(msq[:, :], msq[:, :], c / HD, c * RMS_EPS, ALU.mult, ALU.add))
                    rsqrt(rn[:, :], msq[:, :], HH, (0,))
                if k == "newton2":
                    rsqrt(rn[:, :], msq[:, :], HH, (1, 2))
                if k == "rotate":
                    dve.wait_ge(s_rot, qh + 1)
                    link(nc.vector.tensor_tensor(rot[:, :, :], rot[:, :, :], bcast(rn[:, :], HD), ALU.mult))
                if k == "split":
                    if qh > 0:
                        dve.wait_ge(s_qt, 2 * qh)
                    link(nc.vector.tensor_copy(stk[:, :, 0, :], rot[:, :, :]))
                    link(nc.vector.tensor_tensor(stk[:, :, 3, :], rot[:, :, :], stk[:, :, 0, :], ALU.subtract))
                    st = stk[:, :, :, :].rearrange("p (t h) w d -> p t h w d", t=HT)
                    for w in range(2):
                        nc.vector.tensor_copy(st[:, :, 0:H, 1 + w, :], st[:, :, 0:H, 3 * w, :])
                        last = nc.vector.tensor_copy(st[:, :, H:HEADS, 1 + w, :], st[:, :, H:HEADS, 3 - 3 * w, :])
                    last.then_inc(s_stk, 1)
                if k == "kT":
                    dve.wait_ge(s_kt, qh + 1)
                    at = h * HT * 128
                    for c in range(KVH):
                        last = nc.vector.tensor_copy(kz[32 * c:32 * c + 32, b, c, at:at + HT * 128],
                                                     banks[4].bitcast(fp16)[32 * c:32 * c + 32, 0:HT * 128])
                    last.then_inc(s_kTs, 1)
                if k in ("qT0", "qT1") and qh in BETWEEN:
                    i = int(k[-1])
                    dve.wait_ge(s_qt, 2 * qh + i + 1)
                    t = h * HT + 2 * i
                    nc.vector.tensor_copy(qT[:, b, t:t + 2, :].rearrange("p a b -> p (a b)"), banks[5 + i].bitcast(fp16)).then_inc(s_qTs, 1)
                if ph == "g":
                    if k == "logits":
                        dve.wait_ge(s_lg, qh + 1)
                        rbb = rb[:, :].rearrange("p (o e) -> p o e", o=1).to_broadcast([128, HT, E])
                        nc.vector.tensor_tensor(lg[:, b, h * HT:(h + 1) * HT, :], banks[3][:, 0:HT * E].rearrange("p (t e) -> p t e", e=E),
                                                rbb, ALU.add).then_inc(s_lgs, 1)
                    if k == ("qT1" if qh == 0 else "logits"):
                        dve.wait_ge(s_xh, qh + 1)
                        at = slice(h * HT * 128, (h + 1) * HT * 128)
                        nc.vector.scalar_tensor_tensor(xl[:, b, at], xT[:, :], WSCALE, xh[:, b, at], ALU.mult, ALU.subtract).then_inc(s_xl, 1)

            def router(b, k):
                lgf = lg[:, b, :, :].rearrange("p t e -> p (t e)")
                gt, eq = pair_gt[:, :], pair_eq[:, :]
                if k == "compare":
                    dve.wait_ge(s_lgs, 2 * b + 2)
                    mine = bcast(lgf, E).rearrange("p (t e) f -> p t e f", t=T)
                    other = lg[:, b, :, :].rearrange("p t (o e) -> p t o e", o=1).to_broadcast([128, T, E, E])
                    cube = lambda a: a.rearrange("p (t e f) -> p t e f", t=T, e=E)
                    nc.vector.tensor_tensor(cube(gt), other, mine, ALU.is_gt)
                    link(nc.vector.tensor_tensor(cube(eq), other, mine, ALU.is_equal))
                if k == "max":
                    link(nc.vector.tensor_reduce(mx[:, 0, :], lg[:, b, :, :], AXX, ALU.max))
                    nc.vector.tensor_tensor(lg[:, b, :, :], lg[:, b, :, :], bcast(mx[:, 0, :], E), ALU.subtract).then_inc(s_lx, 1)
                if k == "rank":
                    before = earlier.rearrange("p (o e) -> p o e", o=1).to_broadcast([128, T, E * E])
                    rows = eq.rearrange("p (t e) -> p t e", t=T)
                    link(nc.vector.tensor_tensor(rows, rows, before, ALU.mult))
                    link(nc.vector.tensor_tensor(gt, gt, eq, ALU.add))
                if k == "choose":
                    link(nc.vector.tensor_reduce(rank[:, :], gt.rearrange("p (a f) -> p a f", f=E), AXX, ALU.add))
                    dve.wait_ge(s_le, b + 1)
                    cwf = cw[:, :, :].rearrange("p t e -> p (t e)")
                    link(nc.vector.scalar_tensor_tensor(cwf, rank[:, :], TOPK - 0.5, cwf, ALU.is_lt, ALU.mult))
                if k == "weigh":
                    link(nc.vector.tensor_reduce(mx[:, 0, :], cw[:, :, :], AXX, ALU.add))
                    link(nc.vector.reciprocal(mx[:, 1, :], mx[:, 0, :]))
                    nc.vector.tensor_tensor(cw[:, :, :], cw[:, :, :], bcast(mx[:, 1, :], E), ALU.mult).then_inc(s_cw, 1)
                if k in ("wT0", "wT1"):
                    i = int(k[-1])
                    dve.wait_ge(s_wtp, 2 * b + i + 1)
                    nc.vector.tensor_copy(wT[:, b, i * HT * 128:(i + 1) * HT * 128], SIDE[0:E, :]).then_inc(s_wts, 1)

            def o_normalise(p):
                dve.wait_ge(s_ot, p + 1)
                o = M.rearrange("p (j c d) -> p j c d", j=J, c=KVH)
                link(nc.vector.reciprocal(rec[:, p % 2, :].rearrange("p (j c) -> p j c", j=J), o[:, :, :, HD]))
                nc.vector.tensor_tensor(on[:, p % 2, :].rearrange("p (c j d) -> p j c d", c=KVH, j=J), o[:, :, :, 0:HD],
                                        rec[:, p % 2, :].rearrange("p (j c o) -> p j c o", j=J, o=1).to_broadcast([128, J, KVH, HD]),
                                        ALU.mult).then_inc(s_on, 1)

            def on_evacuate(p):
                dve.wait_ge(s_ont, p + 1)
                nc.vector.tensor_copy(onT[:, p % 2, :], M[:, 0:128]).then_inc(s_ons, 1)

            def residual(p):
                dve.wait_ge(s_wo, p + 1)
                xt = x[:, (p // T) % B, p % T, :]
                nc.vector.tensor_tensor(xt, M[:, 128:256], xt, ALU.add).then_inc(s_x1, 1)

            def global_step(u):
                if u - 2 * LAG in TURNS:
                    residual(TURNS[u - 2 * LAG])
                if u - LAG in TURNS:
                    on_evacuate(TURNS[u - LAG])
                if u in TURNS:
                    o_normalise(TURNS[u])
                if u - 2 in ENDS:
                    p = ENDS[u - 2]
                    dve.wait_ge(s_pv, u - 1)
                    nc.vector.tensor_copy(oT[:, p % 3, :], OB[p % 2]).then_inc(s_o, 1)

            def local_step(lt, k):
                p = B * T + lt - 1
                if 2 <= lt and k == 1:
                    residual(p - 1)
                if 1 <= lt <= B * T:
                    if k == 2:
                        o_normalise(p)
                    if k == 4:
                        on_evacuate(p)

            def ffn(n, part):
                if 1 <= n <= B * HU and part == 0:
                    m = n - 1
                    dve.wait_ge(s_us, m + 1)
                    nc.vector.tensor_scalar(UP[m % 3], UP[m % 3], 1.0 + LIMIT, 1.0 - LIMIT, ALU.min, ALU.max)
                    dve.wait_ge(s_th, m + 1)
                    link(nc.vector.scalar_tensor_tensor(sig[:, m % 2, :], sig[:, m % 2, :], 1.0, gate[:, m % 2, :], ALU.add, ALU.mult))
                    nc.vector.tensor_tensor(UP[m % 3], UP[m % 3], sig[:, m % 2, :], ALU.mult).then_inc(s_a, 1)
                if n < B * HU and part == 1:
                    dve.wait_ge(s_gs, n + 1)
                    nc.vector.tensor_scalar(gate[:, n % 2, :], gate[:, n % 2, :], LIMIT, None, ALU.min).then_inc(s_gm, 1)

            def y_back(g, k):
                if k == 1:
                    c = g % NCH
                    dve.wait_ge(s_yth, g + 1)
                    y = ys[:, c * CH // 128:(c + 1) * CH // 128, :].rearrange("p t d -> p (t d)")
                    nc.vector.scalar_tensor_tensor(y, y, 1.0, Y, ALU.add, ALU.mult).then_inc(s_yd, 1)

            def result(g):
                b, c = divmod(g, NCH)
                ts = slice(c * CH // 128, (c + 1) * CH // 128)
                part = lambda a: a.rearrange("p t d -> p (t d)")
                y = part(ys[:, ts, :])
                dve.wait_ge(s_x1, (B + b) * T + (c + 1) * CH // 128)
                dve.wait_ge(s_yd, g + 1)
                link(nc.vector.scalar_tensor_tensor(y, y, 0.5, part(x[:, b, ts, :]), ALU.mult, ALU.mult))
                nc.vector.tensor_tensor(y, y, part(xs[:, b, ts, :]), ALU.add).then_inc(s_out, 1)

            def first_weights():
                dve.wait_ge(s_pw, 2)
                nc.vector.tensor_copy(kvdT[:, :], SIDE[0:32, 0:128]).then_inc(s_pe_, 1)
                nc.vector.tensor_copy(rwT[:, :], SIDE[:, 192:192 + E]).then_inc(s_pe_, 1)
                projection_weights("g").then_inc(s_pe_, 1)
                dve.wait_ge(s_pw, 3)
                nc.vector.tensor_scalar(wproj["g"][:, H * HD:PROJ], SIDE[:, 128:192], norm_w["g"][:, 0:1], None, ALU.mult).then_inc(s_pe_, 1)

            steps = {"P": first_weights, "Q": qkv, "R": router, "G": global_step, "L": local_step, "F": ffn, "Y": y_back,
                     "W": weights, "O": result}
            for kind, *args in SCHEDULE:
                if kind in steps:
                    steps[kind](*args)


_INS = ["L0_attn_hidden", "L0_attn_norm1_w", "L0_attn_norm2_w", "L0_attn_g_wq", "L0_attn_g_kv_down", "L0_attn_g_k_up",
        "L0_attn_g_v_up", "L0_attn_g_wo", "L0_attn_l_wq", "L0_attn_l_wk", "L0_attn_l_wv", "L0_attn_l_wo",
        "L0_ffn_router_weight", "L0_ffn_router_bias", "L0_ffn_gate_up_proj", "L0_ffn_gate_up_proj_bias",
        "L0_ffn_down_proj", "L0_ffn_down_proj_bias"]


def _constants():
    import numpy as np
    f = np.float32
    parts = [np.eye(128, dtype=f), np.tile(np.tril(np.ones((E, E), f), -1).reshape(1, -1), (128, 1))]
    for base in (1000000.0, 10000.0):
        inv = (f(1.0) / f(base) ** (np.arange(0, HD, 2, dtype=f) / f(HD))).astype(f)
        ang = np.arange(S, dtype=f)[:, None] * inv[None, :]
        cos, sin = np.cos(ang), np.sin(ang)
        for a in (np.stack([cos, cos], -1), np.stack([-sin, sin], -1)):
            parts.append(a.reshape(T, 128, HD).transpose(1, 0, 2).reshape(128, T * HD).astype(f))
    return np.ascontiguousarray(np.concatenate(parts, 1)), np.eye(128, dtype=np.float16)


def kernel(**inputs):
    import numpy as _np
    import concourse.bacc as _bacc
    from concourse import mybir as _mybir
    from concourse.bass_utils import run_bass_kernel_spmd as _run

    nc = _bacc.Bacc("TRN2", target_bir_lowering=False, num_devices=1)
    arrays, args = {}, []
    c32, c16 = _constants()
    for name, a in [(n, _np.ascontiguousarray(inputs[n])) for n in _INS] + [("const32", c32), ("const16", c16)]:
        arrays[f"in_{name}_dram"] = a
        args.append(nc.dram_tensor(f"in_{name}_dram", a.shape, _mybir.dt.from_np(a.dtype), kind="ExternalInput").ap())
    args.append(nc.dram_tensor("out_0_dram", (B, S, D), _mybir.dt.float32, kind="ExternalOutput").ap())
    gated_attention_moe_kernel(nc, *args)
    r = _run(nc, [arrays], core_ids=[0])
    return r.results[0]["out_0_dram"]
```
